# Optimizing a Trainium2 kernel written in Bass

```python
import numpy as np
import jax
import jax.numpy as jnp

def _softmax(x, axis=-1):
    return jax.nn.softmax(x, axis=axis)

def _gelu(x):
    return jax.nn.gelu(x, approximate=True)

def _silu(x):
    return jax.nn.silu(x)

def _sigmoid(x):
    return jax.nn.sigmoid(x)

def _layernorm(x, axis=-1, eps=1e-05):
    m = jnp.mean(x, axis=axis, keepdims=True)
    v = jnp.var(x, axis=axis, keepdims=True)
    return (x - m) / jnp.sqrt(v + eps)

def _scatter_add(tgt, idx, src, axis=0):
    return tgt.at[idx].add(src)

def _segment_sum(src, seg, n):
    return jax.ops.segment_sum(src, seg, n)
kernel_name = 'mk_gnn_preln_d2_gnn_r8_674d9d'

def setup_inputs(seed: int=0):
    np.random.seed(seed)
    _w = jnp.asarray

    def _rec_inputs():
        import jax
        import jax.numpy as jnp
        _gk = jax.random.key(seed)
        x = -0.000202 + 1 * jax.random.normal(jax.random.fold_in(_gk, 1), (12500, 128), jnp.float32)
        src = jax.random.randint(jax.random.fold_in(_gk, 2), (200000,), 0, 12500, jnp.int32)
        dst = jax.random.randint(jax.random.fold_in(_gk, 3), (200000,), 0, 12500, jnp.int32)
        _o = jnp.argsort(dst, stable=True)
        src = src[_o]
        dst = dst[_o]
        edge_attr_16 = 0.000254156 + 0.999948 * jax.random.normal(jax.random.fold_in(_gk, 11), (200000, 16), jnp.float32)
        edge_attr_6 = -0.000118475 + 1.00003 * jax.random.normal(jax.random.fold_in(_gk, 12), (200000, 6), jnp.float32)
        return (x, src, dst, edge_attr_16, edge_attr_6)
    x, src, dst, edge_attr_16, edge_attr_6 = _rec_inputs()

    def _L0_gnn_setup():
        import jax, jax.numpy as jnp
        import numpy as np
        N_NODES = 6250
        N_EDGES = 75000
        NUM_RADIAL = 6
        HIDDEN = 128
        OUT_EMB_HALF = 128
        OUT_CH = 128
        key = jax.random.key(seed)
        ks = jax.random.split(key, 8)
        x = jax.random.normal(ks[0], (N_NODES, HIDDEN), dtype=jnp.float32)
        rbf = jax.random.normal(ks[1], (N_EDGES, NUM_RADIAL), dtype=jnp.float32)
        edge_index = jax.random.randint(ks[2], (2, N_EDGES), 0, N_NODES, dtype=jnp.int64)
        s = 1.0 / np.sqrt(NUM_RADIAL)
        W_rbf = jax.random.uniform(ks[3], (HIDDEN, NUM_RADIAL), jnp.float32, -s, s)
        s1 = 1.0 / np.sqrt(HIDDEN)
        W1 = jax.random.uniform(ks[4], (OUT_EMB_HALF, HIDDEN), jnp.float32, -s1, s1)
        b1 = jax.random.uniform(ks[5], (OUT_EMB_HALF,), jnp.float32, -s1, s1)
        s2 = 1.0 / np.sqrt(OUT_EMB_HALF)
        W2 = jax.random.uniform(ks[6], (OUT_CH, OUT_EMB_HALF), jnp.float32, -s2, s2)
        b2 = jax.random.uniform(ks[7], (OUT_CH,), jnp.float32, -s2, s2)
        return {'x': x, 'rbf': rbf, 'edge_index': edge_index, 'W_rbf': W_rbf, 'W1': W1, 'b1': b1, 'W2': W2, 'b2': b2}
    _L0_gnn_all = _L0_gnn_setup()
    _L0_gnn_in = {k: v for k, v in _L0_gnn_all.items() if k in ('W_rbf', 'W1', 'b1', 'W2', 'b2')}
    del _L0_gnn_all

    def _L1_gnn_setup():
        import jax, jax.numpy as jnp
        import numpy as np
        N = 6250
        IN_DIM = 128
        HIDDEN = 128
        EDGE_DIM = 16
        E = 100000

        def _linear_init(key, fan_in, fan_out):
            kw, kb = jax.random.split(key)
            bound = 1.0 / np.sqrt(fan_in)
            W = jax.random.uniform(kw, (fan_in, fan_out), minval=-bound, maxval=bound, dtype=jnp.float32)
            b = jax.random.uniform(kb, (fan_out,), minval=-bound, maxval=bound, dtype=jnp.float32)
            return (W, b)
        key = jax.random.key(seed)
        k = jax.random.split(key, 8)
        h = jax.random.normal(k[0], (N, IN_DIM), dtype=jnp.float32)
        edge_index = jax.random.randint(k[1], (2, E), 0, N, dtype=jnp.int64)
        edge_feat = jax.random.normal(k[2], (E, EDGE_DIM), dtype=jnp.float32)
        W1, b1 = _linear_init(k[3], 2 * IN_DIM + EDGE_DIM, HIDDEN)
        W2, b2 = _linear_init(k[4], HIDDEN, HIDDEN)
        W3, b3 = _linear_init(k[5], IN_DIM + HIDDEN, HIDDEN)
        W4, b4 = _linear_init(k[6], HIDDEN, HIDDEN)
        return {'h': h, 'edge_index': edge_index, 'edge_feat': edge_feat, 'W1': W1, 'b1': b1, 'W2': W2, 'b2': b2, 'W3': W3, 'b3': b3, 'W4': W4, 'b4': b4}
    _L1_gnn_all = _L1_gnn_setup()
    _L1_gnn_in = {k: v for k, v in _L1_gnn_all.items() if k in ('W1', 'b1', 'W2', 'b2', 'W3', 'b3', 'W4', 'b4')}
    del _L1_gnn_all
    return {'x': x, 'src': src, 'dst': dst, 'edge_attr_16': edge_attr_16, 'edge_attr_6': edge_attr_6, 'L0_gnn_W_rbf': _L0_gnn_in['W_rbf'], 'L0_gnn_W1': _L0_gnn_in['W1'], 'L0_gnn_b1': _L0_gnn_in['b1'], 'L0_gnn_W2': _L0_gnn_in['W2'], 'L0_gnn_b2': _L0_gnn_in['b2'], 'L1_gnn_W1': _L1_gnn_in['W1'], 'L1_gnn_b1': _L1_gnn_in['b1'], 'L1_gnn_W2': _L1_gnn_in['W2'], 'L1_gnn_b2': _L1_gnn_in['b2'], 'L1_gnn_W3': _L1_gnn_in['W3'], 'L1_gnn_b3': _L1_gnn_in['b3'], 'L1_gnn_W4': _L1_gnn_in['W4'], 'L1_gnn_b4': _L1_gnn_in['b4']}

def reference(x, src, dst, edge_attr_16, edge_attr_6, L0_gnn_W_rbf, L0_gnn_W1, L0_gnn_b1, L0_gnn_W2, L0_gnn_b2, L1_gnn_W1, L1_gnn_b1, L1_gnn_W2, L1_gnn_b2, L1_gnn_W3, L1_gnn_b3, L1_gnn_W4, L1_gnn_b4):
    import jax
    import jax.numpy as jnp

    def _L0_gnn_ref(x, rbf, edge_index, W_rbf, W1, b1, W2, b2):
        import jax, jax.numpy as jnp
        import numpy as np
        N_NODES = 6250
        N_EDGES = 75000
        NUM_RADIAL = 6
        HIDDEN = 128
        OUT_EMB_HALF = 128
        OUT_CH = 128
        rbf_emb = rbf @ W_rbf.T
        row, col = (edge_index[0], edge_index[1])
        x_edge = x[row] * rbf_emb
        out = jnp.zeros_like(x).at[col].add(x_edge)
        h = jax.nn.silu(out @ W1.T + b1)
        return h @ W2.T + b2

    def _L1_gnn_ref(h, edge_index, edge_feat, W1, b1, W2, b2, W3, b3, W4, b4):
        import jax, jax.numpy as jnp
        import numpy as np
        N = 6250
        IN_DIM = 128
        HIDDEN = 128
        EDGE_DIM = 16
        E = 100000

        def _linear_init(key, fan_in, fan_out):
            kw, kb = jax.random.split(key)
            bound = 1.0 / np.sqrt(fan_in)
            W = jax.random.uniform(kw, (fan_in, fan_out), minval=-bound, maxval=bound, dtype=jnp.float32)
            b = jax.random.uniform(kb, (fan_out,), minval=-bound, maxval=bound, dtype=jnp.float32)
            return (W, b)
        src, dst = (edge_index[0], edge_index[1])
        msg_input = jnp.concatenate([h[src], h[dst], edge_feat], axis=-1)
        messages = jax.nn.silu(msg_input @ W1 + b1) @ W2 + b2
        agg = jax.ops.segment_sum(messages, dst, num_segments=h.shape[0])
        upd_in = jnp.concatenate([h, agg], axis=-1)
        h_new = jax.nn.silu(upd_in @ W3 + b3) @ W4 + b4
        return h_new + h
    edge_index = jnp.stack([src, dst])
    h = jnp.maximum(_layernorm(x, axis=-1), 0.0)
    x = x + _L0_gnn_ref(h, edge_attr_6, edge_index, L0_gnn_W_rbf, L0_gnn_W1, L0_gnn_b1, L0_gnn_W2, L0_gnn_b2)
    h = jnp.maximum(_layernorm(x, axis=-1), 0.0)
    x = x + _L1_gnn_ref(h, edge_index, edge_attr_16, L1_gnn_W1, L1_gnn_b1, L1_gnn_W2, L1_gnn_b2, L1_gnn_W3, L1_gnn_b3, L1_gnn_W4, L1_gnn_b4)
    return x

_drawn_inputs = setup_inputs


def setup_inputs(seed=0):
    import zlib

    import numpy as np

    out = dict(_drawn_inputs(seed))
    spreads = {}
    factors = {'edge_attr_16': 4.154, 'L0_gnn_b1': 2.891, 'L1_gnn_b1': 3.521, 'L1_gnn_b3': 7.222}
    for name, (base, spread) in spreads.items():
        noise = np.random.default_rng([zlib.crc32(name.encode()), seed]).standard_normal(out[name].shape)
        drawn = base * np.exp(spread * noise) if base else spread * noise
        out[name] = jnp.asarray(drawn.astype(out[name].dtype))
    for name, factor in factors.items():
        out[name] = (out[name] * factor).astype(out[name].dtype)
    return out
```

```python
from contextlib import ExitStack

import numpy as np
import concourse.bass as bass
from concourse import mybir

F32 = mybir.dt.float32
BF16 = mybir.dt.bfloat16
I32 = mybir.dt.int32
ALU = mybir.AluOpType
ACT = mybir.ActivationFunctionType
AX_X = mybir.AxisListType.X

N_NODES, N_EDGES, HID = 12500, 200000, 128
N_RBF, N_EF = 6, 16
LN_EPS = 1e-5
RSQRT_SEED, NEWTON = 0x5F3759DF, 4
P = 128
ROWS = 125
NODE_TILES = N_NODES // ROWS
BT = 4
SPLIT = ROWS // 16 * 16
BN = BT * ROWS
BLOCKS = NODE_TILES // BT
PIECES = 5
PIECE_TILES = NODE_TILES // PIECES
PIECE_BLOCKS = BLOCKS // PIECES
K = 8
CHUNK = K * P
FULL = N_EDGES // CHUNK
TAIL = N_EDGES - FULL * CHUNK
TAIL_K = 4
TAIL_ROWS = TAIL // TAIL_K
N_CHUNKS = FULL + 1
RING = 4
GROUPS = N_CHUNKS // RING
WINDOW = P - N_EF
MIN_P = FULL // 3
assert TAIL_K * TAIL_ROWS == TAIL and GROUPS * RING == N_CHUNKS and MIN_P * 3 == FULL


def gnn_kernel(nc, x, dst, ids, ids_tail, rbf, rbf_tail, ef, ef_tail, w_rbf_t, w1_t, b1, w2_t, b2,
               m1, mb1, m2, mb2, m3, mb3, m4, mb4, out):
    h_table = nc.dram_tensor("h_table", (N_NODES, HID), F32).ap()
    a_table = nc.dram_tensor("a_table", (N_NODES, HID), F32).ap()
    b_table = nc.dram_tensor("b_table", (N_NODES + WINDOW, HID), F32).ap()
    lo_table = nc.dram_tensor("lo_table", (1, N_CHUNKS), F32).ap()
    hi_table = nc.dram_tensor("hi_table", (1, N_CHUNKS), F32).ap()

    with ExitStack() as ctx:
        def sb(name, shape, dt=F32):
            return ctx.enter_context(nc.sbuf_tensor(name, shape, dt))

        def sem(name):
            return ctx.enter_context(nc.semaphore(name))

        def sems(name, n):
            return [sem(f"{name}{i}") for i in range(n)]

        acc = sb("acc", [P, N_NODES + WINDOW])
        node_x = sb("node_x", [ROWS, NODE_TILES * HID])
        node_h = sb("node_h", [ROWS, NODE_TILES * HID])
        gath = sb("gath", [P, RING, K, HID])
        lhs = sb("lhs", [P, RING, CHUNK])
        onehot = sb("onehot", [P, 2, K, WINDOW])
        win_b = sb("win_b", [P, RING, HID])
        idst = sb("idst", [P, RING, 2 * K], I32)
        rel = sb("rel", [P, 2, K])
        iota_w = sb("iota_w", [P, WINDOW])
        chunk_lo = sb("chunk_lo", [P, N_CHUNKS])
        win_lo = sb("win_lo", [P, N_CHUNKS])
        base_i = sb("base_i", [1, N_CHUNKS], I32)
        hi_row = sb("hi_row", [1, N_CHUNKS])
        lo3 = sb("lo3", [MIN_P, 3])
        hi3 = sb("hi3", [MIN_P, 3])
        lo_t = sb("lo_t", [1, 1])
        hi_t = sb("hi_t", [1, 1])
        span = sb("span", [1, N_CHUNKS])
        span_max = sb("span_max", [1, 1])
        span_i = sb("span_i", [1, 1], I32)
        sums = sb("sums", [P, WINDOW])
        sums2 = sb("sums2", [P, WINDOW])
        deg = sb("deg", [1, WINDOW])
        ident = sb("ident", [P, P])
        ident_h = sb("ident_h", [P, P], BF16)
        ones_h = sb("ones_h", [P, 1], BF16)
        stats = sb("stats", [ROWS, BT, 6])
        mv = sb("mv", [ROWS, BT, 2])
        neg_mean = sb("neg_mean", [ROWS, NODE_TILES])
        var_eps = sb("var_eps", [ROWS, NODE_TILES])
        neg_half_var = sb("neg_half_var", [ROWS, NODE_TILES])
        three_halves = sb("three_halves", [ROWS, BT])
        seed = sb("seed", [ROWS, NODE_TILES], I32)
        newton = sb("newton", [ROWS, NODE_TILES])
        rstd = sb("rstd", [ROWS, NODE_TILES])
        nmr = sb("nmr", [ROWS, NODE_TILES])
        w_rbf_s = sb("w_rbf_s", [N_RBF, HID])
        w1_s = sb("w1_s", [P, HID])
        w2_s = sb("w2_s", [P, HID])
        m1ab_s = sb("m1ab_s", [P, 2, HID])
        m2_s = sb("m2_s", [P, HID])
        m3a_s = sb("m3a_s", [P, HID])
        m3b_s = sb("m3b_s", [P, HID])
        m4_s = sb("m4_s", [P, HID])
        b1_s = sb("b1_s", [P, 1])
        mb3_s = sb("mb3_s", [P, 1])
        b2_s = sb("b2_s", [ROWS, HID])
        mb1_s = sb("mb1_s", [ROWS, HID])
        mb4_s = sb("mb4_s", [ROWS, HID])
        mb2_s = sb("mb2_s", [1, HID])
        psum = ctx.enter_context(nc.psum_tensor("psum", [P, 8, 512], F32))

        gflat = gath[:, :, :, :].rearrange("p r k f -> p (r k f)")
        dst3 = gflat[0:MIN_P, 0:3 * CHUNK].bitcast(I32).rearrange("p (k e) -> p k e", k=3)
        dst_t = gflat[0:1, 3 * CHUNK:3 * CHUNK + TAIL].bitcast(I32)
        lflat = lhs[:, :, :].rearrange("p r e -> p (r e)")
        u_buf = lflat[:, 0:BN]
        ht_buf = lflat[:, CHUNK:CHUNK + BN]
        h_buf = lflat[0:ROWS, 2 * CHUNK:2 * CHUNK + BT * HID]
        b_stage = gflat[0:ROWS, 0:BT * HID]
        zeros = onehot[:, :, :, :].rearrange("p a k w -> p (a k w)")[0:WINDOW, 0:HID]
        ps_pre = psum[:, 0:2, :].rearrange("p a (k f) -> p (a k) f", f=HID)
        ps_oht = psum[:, 2, :].bitcast(BF16)
        ps_sum = psum[:, 3, 0:WINDOW]
        ps_deg = psum[0:1, 3, 256:256 + WINDOW]
        ps_proj = psum[:, 4, 0:WINDOW]
        ps_proj2 = psum[:, 5, 0:WINDOW]
        ps_w = psum[0:ROWS, 0, :]
        ps_t = psum[:, 1, 0:BN]
        ps_ab = psum[0:ROWS, 2:4, :].rearrange("p a (k f) -> p (a k) f", f=2 * HID)
        ps_c = psum[:, 4, 0:BN]

        def node_tiles(ap, j0, n):
            return ap[:, bass.ds(j0 * HID, n * HID)]

        def table_rows(t, j0, n):
            return t[bass.ds(j0 * ROWS, n * ROWS), :].rearrange("(j p) f -> p j f", p=ROWS)

        waited = {name: sem(f"waited_{name}") for name in ("dve", "pool", "sp")}
        x_loaded = sems("x_loaded", PIECES)
        dst_loaded = sem("dst_loaded")
        weights_loaded = sem("weights_loaded")
        extremes_ready = sem("extremes_ready")
        extremes_stored = sem("extremes_stored")
        extremes_loaded = sem("extremes_loaded")
        span_steps = sem("span_steps")
        span_ready = sem("span_ready")
        consts_ready = sem("consts_ready")
        ident_zero = sem("ident_zero")
        ident_ready = sem("ident_ready")
        acc_zeroed = sem("acc_zeroed")
        zeros_ready = sem("zeros_ready")
        zeros_stored = sem("zeros_stored")
        bn_done = sem("bn_done")
        stats_ready = sem("stats_ready")
        rstd_step = sem("rstd_step")
        norm_ready = sem("norm_ready")
        h_ready = sem("h_ready")
        h_stored = sem("h_stored")
        bias_added = sem("bias_added")
        summed = sems("summed", 2)
        ids_loaded = [sems(f"ids_loaded{l}_", RING) for l in range(2)]
        feats_loaded = [sems(f"feats_loaded{l}_", RING) for l in range(2)]
        gathered = [sems(f"gathered{l}_", RING) for l in range(2)]
        window_step = sems("window_step", 2)
        window_ready = sems("window_ready", 2)
        rel_ready = sems("rel_ready", 2)
        onehot_ready = sems("onehot_ready", 2)
        turned = sem("turned")
        turned_copied = sem("turned_copied")
        products_ready = sems("products_ready", 2)
        mixed = sems("mixed", 2)
        messages_ready = sem("messages_ready")
        sums_copied = sems("sums_copied", 2)
        projected = sems("projected", 2)
        projection_copied = sem("projection_copied")
        updated = sem("updated")
        acc_added = sems("acc_added", 2)
        u_ready = sem("u_ready")
        w2_done = sem("w2_done")
        x2_ready = sem("x2_ready")
        bn2_done = sem("bn2_done")
        stats2_ready = sem("stats2_ready")
        rstd2_step = sem("rstd2_step")
        norm2_ready = sem("norm2_ready")
        h2_ready = sem("h2_ready")
        xh_ready = sem("xh_ready")
        ht_ready = sem("ht_ready")
        ht_copied = sem("ht_copied")
        abc_done = sem("abc_done")
        a_ready = sem("a_ready")
        b_ready = sem("b_ready")
        c_ready = sem("c_ready")
        a_stored = sem("a_stored")
        b_stored = sem("b_stored")
        v_ready = sem("v_ready")
        w4_done = sem("w4_done")
        y_ready = sem("y_ready")
        out_stored = sem("out_stored")

        N_WEIGHTS = 15 + RING

        def sweeps(eng):
            eng.wait_ge(span_ready, 1)
            widest = eng.value_load(span_i[0:1, 0:1], min_val=0, max_val=N_NODES - 1)
            return widest // WINDOW + 1

        def shape_of(i, r):
            return (TAIL_K, TAIL_ROWS) if i is LAST and r == RING - 1 else (K, P)

        LAST = "last"

        def number(i):
            return GROUPS - 1 if i is LAST else i

        def gathered_count(q, i, r):
            per_sweep = 16 * (K * (GROUPS - 1) + shape_of(LAST, r)[0])
            return q * per_sweep + 16 * K * number(i) + 16 * shape_of(i, r)[0]

        block = ctx.enter_context(nc.Block())

        @block.sync
        def _(sp):
            def load_nodes(tile, table, j0, n, done):
                dram = table_rows(table, j0, n)
                on_chip = tile.rearrange("p (j f) -> p j f", f=HID)
                for lo, hi in ((0, SPLIT), (SPLIT, ROWS)):
                    sp.dma_start(on_chip[lo:hi], dram[lo:hi]).then_inc(done, 16)

            def store_nodes(table, j0, n, tile, done):
                dram = table_rows(table, j0, n)
                on_chip = tile.rearrange("p (j f) -> p j f", f=HID)
                for lo, hi in ((0, SPLIT), (SPLIT, ROWS)):
                    sp.dma_start(dram[lo:hi], on_chip[lo:hi]).then_inc(done, 16)

            sp.dma_start(dst3, dst[0:FULL * CHUNK].rearrange("(p k e) -> p k e", k=3, e=CHUNK)
                         ).then_inc(dst_loaded, 16)
            sp.dma_start(dst_t, dst[FULL * CHUNK:N_EDGES].rearrange("(a e) -> a e", a=1)).then_inc(dst_loaded, 16)
            for n in range(PIECES):
                load_nodes(node_tiles(node_x, n * PIECE_TILES, PIECE_TILES), x, n * PIECE_TILES, PIECE_TILES,
                           x_loaded[n])
            for tile, src in ((w_rbf_s[:, :], w_rbf_t), (w1_s[:, :], w1_t), (w2_s[:, :], w2_t),
                              (m1ab_s[:, 0, :], m1[0:HID, :]), (m1ab_s[:, 1, :], m1[HID:2 * HID, :]),
                              (m2_s[:, :], m2), (m3a_s[:, :], m3[0:HID, :]), (m3b_s[:, :], m3[HID:2 * HID, :]),
                              (m4_s[:, :], m4), (b1_s[:, :], b1), (mb3_s[:, :], mb3), (mb2_s[:, :], mb2),
                              (b2_s[:, :], b2.partition_broadcast(ROWS)), (mb1_s[:, :], mb1.partition_broadcast(ROWS)),
                              (mb4_s[:, :], mb4.partition_broadcast(ROWS))):
                sp.dma_start(tile, src).then_inc(weights_loaded, 16)
            for r in range(RING):
                sp.dma_start(win_b[WINDOW:P, r, :], m1[2 * HID:2 * HID + N_EF, :]).then_inc(weights_loaded, 16)
            sp.wait_ge(extremes_ready, 4)
            sp.dma_start(lo_table[0, 0:FULL].rearrange("(p k) -> p k", k=3), lo3[:, :]).then_inc(extremes_stored, 16)
            sp.dma_start(hi_table[0, 0:FULL].rearrange("(p k) -> p k", k=3), hi3[:, :]).then_inc(extremes_stored, 16)
            sp.dma_start(lo_table[:, FULL:N_CHUNKS], lo_t[:, :]).then_inc(extremes_stored, 16)
            sp.dma_start(hi_table[:, FULL:N_CHUNKS], hi_t[:, :]).then_inc(extremes_stored, 16)
            sp.wait_ge(extremes_stored, 64)
            sp.dma_start(chunk_lo[:, :], lo_table.partition_broadcast(P)).then_inc(extremes_loaded, 16)
            sp.dma_start(hi_row[:, :], hi_table).then_inc(extremes_loaded, 16)
            sp.wait_ge(zeros_ready, 1)
            sp.dma_start(b_table[N_NODES:N_NODES + WINDOW, :], zeros).then_inc(zeros_stored, 16)
            for n in range(PIECES):
                sp.wait_ge(h_ready, PIECE_BLOCKS * (n + 1))
                store_nodes(h_table, n * PIECE_TILES, PIECE_TILES, node_tiles(node_h, n * PIECE_TILES, PIECE_TILES),
                            h_stored)

            n_sweeps = sweeps(sp)

            def load_group(layer, q, i):
                for r in range(RING):
                    k, rows = shape_of(i, r)
                    c = RING * number(i) + r
                    sp.wait_ge(summed[layer], q * N_CHUNKS + c + 1)
                    tail = k != K
                    ids_src = ids_tail if tail else ids[bass.ds(c * P, P), :]
                    sp.dma_start(idst[0:rows, r, 0:2 * k], ids_src).then_inc(ids_loaded[layer][r], 16)
                    if layer == 0:
                        src = rbf_tail if tail else rbf[bass.ds(c * N_RBF, N_RBF), :]
                        sp.dma_start(lhs[0:N_RBF, r, 0:k * rows], src).then_inc(feats_loaded[0][r], 16)
                    else:
                        src = ef_tail if tail else ef[bass.ds(c * N_EF, N_EF), :]
                        sp.dma_start(lhs[WINDOW:P, r, 0:k * rows], src).then_inc(feats_loaded[1][r], 16)
                        base = sp.value_load(base_i[0:1, bass.ds(c, 1)], min_val=0, max_val=N_NODES)
                        sp.dma_start(win_b[0:WINDOW, r, :], b_table[bass.ds(base, WINDOW), :]
                                     ).then_inc(feats_loaded[1][r], 16)

            with sp.Fori(0, n_sweeps) as q:
                with sp.Fori(0, GROUPS - 1) as i:
                    load_group(0, q, i)
                load_group(0, q, LAST)

            def store_ab(j):
                sp.wait_ge(a_ready, j + 1)
                store_nodes(a_table, j * BT, BT, node_tiles(node_h, j * BT, BT), a_stored)
                sp.wait_ge(b_ready, j + 1)
                store_nodes(b_table, j * BT, BT, b_stage, b_stored)

            with sp.Fori(0, BLOCKS) as j:
                store_ab(j)
            sp.wait_ge(b_stored, 32 * BLOCKS)
            sp.wait_ge(a_stored, 32 * BLOCKS)
            sp.wait_ge(zeros_stored, 16)

            with sp.Fori(0, n_sweeps) as q:
                sp.wait_ge(window_ready[1], q + 1)
                sp.sem_inc(waited["sp"], 1)
                with sp.Fori(0, GROUPS - 1) as i:
                    load_group(1, q, i)
                load_group(1, q, LAST)

            for n in range(PIECES):
                sp.wait_ge(y_ready, PIECE_BLOCKS * (n + 1))
                store_nodes(out, n * PIECE_TILES, PIECE_TILES, node_tiles(node_x, n * PIECE_TILES, PIECE_TILES),
                            out_stored)
            sp.wait_ge(out_stored, 32 * PIECES)
            sp.wait_ge(h_stored, 32 * PIECES)
            sp.wait_ge(weights_loaded, 16 * N_WEIGHTS)

        @block.gpsimd
        def _(pool):
            nc.gpsimd.iota(iota_w[:, :], pattern=[[1, WINDOW]], base=0, channel_multiplier=0,
                           allow_small_or_imprecise_dtypes=True).then_inc(consts_ready, 1)
            nc.gpsimd.memset(ones_h[:, :], 1.0).then_inc(consts_ready, 1)
            nc.gpsimd.memset(three_halves[:, :], 1.5).then_inc(consts_ready, 1)
            nc.gpsimd.memset(ident[:, :], 0.0).then_inc(ident_zero, 1)
            nc.gpsimd.memset(ident_h[:, :], 0.0).then_inc(ident_zero, 1)
            nc.gpsimd.memset(zeros, 0.0).then_inc(zeros_ready, 1)
            pool.wait_ge(ident_zero, 2)
            nc.gpsimd.affine_select(out=ident[:, :], in_=ident[:, :], compare_op=ALU.not_equal, fill=1.0,
                                    base=0, pattern=[[-1, P]], channel_multiplier=1).then_inc(ident_ready, 1)
            nc.gpsimd.affine_select(out=ident_h[:, :], in_=ident_h[:, :], compare_op=ALU.not_equal, fill=1.0,
                                    base=0, pattern=[[-1, P]], channel_multiplier=1).then_inc(ident_ready, 1)

            def rstd_of(j, ready, step, done):
                cols = bass.ds(j * BT, BT)
                y, t, v = rstd[:, cols], newton[:, cols], neg_half_var[:, cols]
                pool.wait_ge(ready, j + 1)
                pool.sem_inc(waited["pool"], 1)
                steps = 4 * NEWTON
                for n in range(NEWTON):
                    if n:
                        pool.wait_ge(step, steps * j + 4 * n)
                        pool.sem_inc(waited["pool"], 1)
                    nc.gpsimd.tensor_tensor(t, y, y, ALU.mult).then_inc(step, 1)
                    pool.wait_ge(step, steps * j + 4 * n + 1)
                    pool.sem_inc(waited["pool"], 1)
                    nc.gpsimd.tensor_tensor(t, t, v, ALU.mult).then_inc(step, 1)
                    pool.wait_ge(step, steps * j + 4 * n + 2)
                    pool.sem_inc(waited["pool"], 1)
                    nc.gpsimd.tensor_tensor(t, t, three_halves[:, :], ALU.add).then_inc(step, 1)
                    pool.wait_ge(step, steps * j + 4 * n + 3)
                    pool.sem_inc(waited["pool"], 1)
                    nc.gpsimd.tensor_tensor(y, y, t, ALU.mult).then_inc(step, 1)
                pool.wait_ge(step, steps * (j + 1))
                pool.sem_inc(waited["pool"], 1)
                nc.gpsimd.tensor_tensor(nmr[:, cols], neg_mean[:, cols], y, ALU.mult).then_inc(done, 1)

            pool.wait_ge(consts_ready, 3)
            with pool.Fori(0, BLOCKS) as j:
                rstd_of(j, stats_ready, rstd_step, norm_ready)
            nc.gpsimd.memset(acc[:, :], 0.0).then_inc(acc_zeroed, 1)

            n_sweeps = sweeps(pool)

            def gather_group(layer, table, q, i):
                for r in range(RING):
                    k, rows = shape_of(i, r)
                    pool.wait_ge(ids_loaded[layer][r], 16 * (q * GROUPS + number(i) + 1))
                    pool.sem_inc(waited["pool"], 1)
                    for t in range(k):
                        pool.indirect_dma_start(
                            out=gath[0:rows, r, t, :], out_offset=None, in_=table,
                            in_offset=bass.IndirectOffsetOnAxis(ap=idst[0:rows, r, t:t + 1], axis=0),
                        ).then_inc(gathered[layer][r], 16)

            pool.wait_ge(h_stored, 32 * PIECES)
            with pool.Fori(0, n_sweeps) as q:
                with pool.Fori(0, GROUPS - 1) as i:
                    gather_group(0, h_table, q, i)
                gather_group(0, h_table, q, LAST)

            def residual(j):
                pool.wait_ge(h2_ready, j + 1)
                pool.sem_inc(waited["pool"], 1)
                xb = node_tiles(node_x, j * BT, BT)
                nc.gpsimd.tensor_tensor(xb, xb, h_buf, ALU.add).then_inc(xh_ready, 1)

            rstd_of(0, stats2_ready, rstd2_step, norm2_ready)
            with pool.Fori(1, BLOCKS) as j:
                rstd_of(j, stats2_ready, rstd2_step, norm2_ready)
                residual(j - 1)
            residual(BLOCKS - 1)

            pool.wait_ge(a_stored, 32 * BLOCKS)
            with pool.Fori(0, n_sweeps) as q:
                with pool.Fori(0, GROUPS - 1) as i:
                    gather_group(1, a_table, q, i)
                gather_group(1, a_table, q, LAST)

        @block.scalar
        def _(act):
            def normalise(j, ready, into, done):
                act.wait_ge(ready, j + 1)
                for t in range(BT):
                    col = bass.ds(j * BT + t, 1)
                    last = nc.scalar.activation(into(t), node_tiles(node_x, j * BT + t, 1), ACT.Relu, bias=nmr[:, col], scale=rstd[:, col])
                last.then_inc(done, 1)

            act.wait_ge(weights_loaded, 16 * N_WEIGHTS)
            with act.Fori(0, BLOCKS) as j:
                normalise(j, norm_ready, lambda t: node_tiles(node_h, j * BT + t, 1), h_ready)

            n_sweeps = sweeps(act)

            def copy_sums(layer, g):
                act.wait_ge(summed[layer], RING + g + 1)
                if layer == 1:
                    nc.scalar.copy(deg[:, :], ps_deg)
                nc.scalar.copy(sums[:, :], ps_sum).then_inc(sums_copied[layer], 1)

            with act.Fori(0, n_sweeps) as q:
                with act.Fori(0, N_CHUNKS) as c:
                    copy_sums(0, q * N_CHUNKS + c)

            def normalise2(j):
                act.wait_ge(ht_ready, j)
                act.wait_ge(xh_ready, j)
                normalise(j, norm2_ready, lambda t: h_buf[:, t * HID:(t + 1) * HID], h2_ready)

            def silu_u(j):
                act.wait_ge(w2_done, j)
                nc.scalar.activation(u_buf, acc[:, bass.ds(j * BN, BN)], ACT.Silu, bias=b1_s[:, 0:1]
                                     ).then_inc(u_ready, 1)

            def keep_c(j):
                act.wait_ge(abc_done, j + 1)
                nc.scalar.activation(acc[:, bass.ds(j * BN, BN)], ps_c, ACT.Identity, bias=mb3_s[:, 0:1]
                                     ).then_inc(c_ready, 1)

            def copy_ht(j):
                act.wait_ge(abc_done, j)
                act.wait_ge(ht_ready, j + 1)
                nc.scalar.copy(ht_buf, ps_t).then_inc(ht_copied, 1)

            act.wait_ge(acc_added[0], n_sweeps * N_CHUNKS)
            silu_u(0)
            silu_u(1)
            normalise2(0)
            silu_u(2)
            copy_ht(0)
            with act.Fori(2, BLOCKS - 1) as j:
                normalise2(j - 1)
                silu_u(j + 1)
                keep_c(j - 2)
                copy_ht(j - 1)
            normalise2(BLOCKS - 2)
            keep_c(BLOCKS - 3)
            copy_ht(BLOCKS - 2)
            normalise2(BLOCKS - 1)
            keep_c(BLOCKS - 2)
            copy_ht(BLOCKS - 1)
            keep_c(BLOCKS - 1)

            def copy_turned(q, i, r):
                k, rows = shape_of(i, r)
                g = q * N_CHUNKS + RING * number(i) + r
                act.wait_ge(feats_loaded[1][r], 32 * (q * GROUPS + number(i) + 1))
                act.wait_ge(turned, g + 1)
                nc.scalar.copy(lhs[0:WINDOW, r, 0:k * rows], ps_oht[0:WINDOW, 0:k * rows]).then_inc(turned_copied, 1)

            def silu_messages(q, i, r):
                k, rows = shape_of(i, r)
                g = q * N_CHUNKS + RING * number(i) + r
                act.wait_ge(mixed[1], g + 1)
                nc.scalar.activation(gath[0:rows, r, 0:k, :], gath[0:rows, r, 0:k, :], ACT.Silu
                                     ).then_inc(messages_ready, 1)
                copy_sums(1, g)
                act.wait_ge(projected[1], g + 1)
                nc.scalar.copy(sums2[:, :], ps_proj).then_inc(projection_copied, 1)

            with act.Fori(0, n_sweeps) as q:
                copy_turned(q, 0, 0)
                with act.Fori(0, GROUPS - 2) as i:
                    for r in range(RING):
                        copy_turned(q, *((i, r + 1) if r + 1 < RING else (i + 1, 0)))
                        silu_messages(q, i, r)
                for r in range(RING):
                    copy_turned(q, *((GROUPS - 2, r + 1) if r + 1 < RING else (LAST, 0)))
                    silu_messages(q, GROUPS - 2, r)
                for r in range(RING):
                    if r + 1 < RING:
                        copy_turned(q, LAST, r + 1)
                    silu_messages(q, LAST, r)

            act.wait_ge(acc_added[1], n_sweeps * N_CHUNKS)
            with act.Fori(0, PIECES) as n:
                for m in range(PIECE_BLOCKS):
                    j = n * PIECE_BLOCKS + m
                    if m == 0:
                        act.wait_ge(w4_done, j)
                    nc.scalar.activation(lflat[:, m * BN:(m + 1) * BN], acc[:, bass.ds(j * BN, BN)], ACT.Silu
                                         ).then_inc(v_ready, 1)

        @block.vector
        def _(dve):
            dve.wait_ge(dst_loaded, 32)
            nc.vector.tensor_reduce(lo3[:, :], dst3, AX_X, ALU.min).then_inc(extremes_ready, 1)
            nc.vector.tensor_reduce(hi3[:, :], dst3, AX_X, ALU.max).then_inc(extremes_ready, 1)
            nc.vector.tensor_reduce(lo_t[:, :], dst_t, AX_X, ALU.min).then_inc(extremes_ready, 1)
            nc.vector.tensor_reduce(hi_t[:, :], dst_t, AX_X, ALU.max).then_inc(extremes_ready, 1)

            def moments(j, bn, done):
                bn_steps = 2 * BT + 2
                for t in range(BT):
                    nc.vector.bn_stats(stats[:, t, :], node_tiles(node_x, j * BT + t, 1)).then_inc(bn, 1)
                dve.wait_ge(bn, bn_steps * j + BT)
                dve.sem_inc(waited["dve"], 1)
                for t in range(BT):
                    nc.vector.bn_aggr(mv[:, t, :], stats[:, t, :]).then_inc(bn, 1)
                cols = bass.ds(j * BT, BT)
                dve.wait_ge(bn, bn_steps * j + 2 * BT)
                nc.vector.tensor_scalar(neg_mean[:, cols], mv[:, :, 0], -1.0, None, ALU.mult)
                nc.vector.tensor_scalar(neg_half_var[:, cols], mv[:, :, 1], LN_EPS, -0.5, ALU.add, ALU.mult)
                nc.vector.tensor_scalar(var_eps[:, cols], mv[:, :, 1], LN_EPS, None, ALU.add).then_inc(bn, 1)
                dve.wait_ge(bn, bn_steps * j + 2 * BT + 1)
                nc.vector.tensor_scalar(seed[:, cols], var_eps[:, cols].bitcast(I32), 1, None,
                                        ALU.logical_shift_right).then_inc(bn, 1)
                dve.wait_ge(bn, bn_steps * (j + 1))
                nc.vector.tensor_scalar(rstd[:, cols].bitcast(I32), seed[:, cols], -1, RSQRT_SEED,
                                        ALU.mult, ALU.add).then_inc(done, 1)

            for n in range(PIECES):
                dve.wait_ge(x_loaded[n], 32)
                with dve.Fori(n * PIECE_BLOCKS, (n + 1) * PIECE_BLOCKS) as j:
                    moments(j, bn_done, stats_ready)

            dve.wait_ge(extremes_loaded, 32)
            nc.vector.tensor_tensor(span[:, :], hi_row[:, :], chunk_lo[0:1, :], ALU.subtract).then_inc(span_steps, 1)
            dve.wait_ge(span_steps, 1)
            nc.vector.tensor_reduce(span_max[:, :], span[:, :], AX_X, ALU.max).then_inc(span_steps, 1)
            dve.wait_ge(span_steps, 2)
            nc.vector.tensor_copy(span_i[:, :], span_max[:, :]).then_inc(span_ready, 1)

            dve.wait_ge(weights_loaded, 16 * N_WEIGHTS)
            for n in range(PIECES):
                dve.wait_ge(h_ready, PIECE_BLOCKS * (n + 1))
                xv = node_tiles(node_x, n * PIECE_TILES, PIECE_TILES).rearrange("p (j f) -> p j f", f=HID)
                nc.vector.tensor_tensor(xv, xv, b2_s[:, :].unsqueeze(1).broadcast_to([ROWS, PIECE_TILES, HID]),
                                        ALU.add).then_inc(bias_added, 1)

            n_sweeps = sweeps(dve)

            def base_row(layer):
                nc.vector.tensor_scalar(base_i[:, :], win_lo[0:1, :], float(N_NODES), None, ALU.min
                                        ).then_inc(window_ready[layer], 1)

            def build_onehot(layer, q, i, r, chunks_summed):
                k, rows = shape_of(i, r)
                c = RING * number(i) + r
                dve.wait_ge(ids_loaded[layer][r], 16 * (q * GROUPS + number(i) + 1))
                nc.vector.tensor_scalar(rel[0:rows, r % 2, 0:k], idst[0:rows, r, k:2 * k],
                                        win_lo[0:rows, bass.ds(c, 1)], None, ALU.subtract).then_inc(rel_ready[layer], 1)
                dve.wait_ge(summed[layer], RING + chunks_summed)
                dve.wait_ge(rel_ready[layer], q * N_CHUNKS + c + 1)
                nc.vector.tensor_tensor(onehot[0:rows, r % 2, 0:k, :],
                                        rel[0:rows, r % 2, 0:k].unsqueeze(2).broadcast_to([rows, k, WINDOW]),
                                        iota_w[0:rows, :].unsqueeze(1).broadcast_to([rows, k, WINDOW]),
                                        ALU.is_equal).then_inc(onehot_ready[layer], 1)

            def mix_and_add(layer, q, i, r):
                k, rows = shape_of(i, r)
                c = RING * number(i) + r
                g = q * N_CHUNKS + c
                dve.wait_ge(products_ready[layer], g + 1)
                dve.wait_ge(gathered[layer][r], gathered_count(q, i, r))
                gv = gath[0:rows, r, 0:k, :]
                nc.vector.tensor_tensor(gv, gv, ps_pre[0:rows, 0:k, :], ALU.add if layer else ALU.mult
                                        ).then_inc(mixed[layer], 1)
                base = dve.value_load(base_i[0:1, bass.ds(c, 1)], min_val=0, max_val=N_NODES)
                dve.wait_ge(updated if layer else projected[0], g + 1)
                dve.wait_ge(acc_added[layer], g)
                av = acc[:, bass.ds(base, WINDOW)]
                nc.vector.tensor_tensor(av, av, ps_proj2 if layer else ps_proj, ALU.add
                                        ).then_inc(acc_added[layer], 1)

            def edge_sweeps(layer):
                nc.vector.tensor_copy(win_lo[:, :], chunk_lo[:, :]).then_inc(window_step[layer], 1)
                dve.wait_ge(window_step[layer], 1)
                base_row(layer)
                with dve.Fori(0, n_sweeps) as q:
                    dve.wait_ge(window_ready[layer], q + 1)
                    build_onehot(layer, q, 0, 0, q * N_CHUNKS)
                    with dve.Fori(0, GROUPS - 2) as i:
                        for r in range(RING):
                            g = q * N_CHUNKS + i * RING + r
                            build_onehot(layer, q, *((i, r + 1) if r + 1 < RING else (i + 1, 0)), g)
                            mix_and_add(layer, q, i, r)
                    for r in range(RING):
                        g = q * N_CHUNKS + (GROUPS - 2) * RING + r
                        build_onehot(layer, q, *((GROUPS - 2, r + 1) if r + 1 < RING else (LAST, 0)), g)
                        mix_and_add(layer, q, GROUPS - 2, r)
                    for r in range(RING):
                        g = q * N_CHUNKS + (GROUPS - 1) * RING + r
                        if r + 1 < RING:
                            build_onehot(layer, q, LAST, r + 1, g)
                        mix_and_add(layer, q, LAST, r)
                    dve.wait_ge(acc_added[layer], (q + 1) * N_CHUNKS)
                    nc.vector.tensor_scalar(win_lo[:, :], win_lo[:, :], float(WINDOW), None, ALU.add
                                            ).then_inc(window_step[layer], 1)
                    dve.wait_ge(window_step[layer], q + 2)
                    base_row(layer)

            dve.wait_ge(consts_ready, 3)
            dve.wait_ge(acc_zeroed, 1)
            dve.wait_ge(zeros_stored, 16)
            edge_sweeps(0)

            def add_x2(j):
                dve.wait_ge(w2_done, j + 1)
                if isinstance(j, int) and j == 0:
                    dve.wait_ge(bias_added, PIECES)
                xb = node_tiles(node_x, j * BT, BT)
                nc.vector.tensor_tensor(xb, xb, ps_w, ALU.add).then_inc(x2_ready, 1)
                dve.wait_ge(x2_ready, j + 1)
                dve.sem_inc(waited["dve"], 1)
                moments(j, bn2_done, stats2_ready)

            def keep_ab(j):
                dve.wait_ge(abc_done, j + 1)
                nc.vector.tensor_copy(node_tiles(node_h, j * BT, BT).rearrange("p (j f) -> p j f", f=HID),
                                      ps_ab[:, :, 0:HID]).then_inc(a_ready, 1)
                dve.wait_ge(b_stored, 32 * j)
                nc.vector.tensor_tensor(b_stage.rearrange("p (j f) -> p j f", f=HID), ps_ab[:, :, HID:2 * HID],
                                        mb1_s[:, :].unsqueeze(1).broadcast_to([ROWS, BT, HID]), ALU.add
                                        ).then_inc(b_ready, 1)

            add_x2(0)
            add_x2(1)
            with dve.Fori(2, BLOCKS) as j:
                add_x2(j)
                keep_ab(j - 2)
            keep_ab(BLOCKS - 2)
            keep_ab(BLOCKS - 1)

            dve.wait_ge(c_ready, BLOCKS)
            dve.wait_ge(xh_ready, BLOCKS)
            for n in range(PIECES):
                xv = node_tiles(node_x, n * PIECE_TILES, PIECE_TILES).rearrange("p (j f) -> p j f", f=HID)
                nc.vector.tensor_tensor(xv, xv, mb4_s[:, :].unsqueeze(1).broadcast_to([ROWS, PIECE_TILES, HID]),
                                        ALU.add).then_inc(bias_added, 1)
            dve.wait_ge(bias_added, 2 * PIECES)
            edge_sweeps(1)

            with dve.Fori(0, PIECES) as n:
                for m in range(PIECE_BLOCKS):
                    j = n * PIECE_BLOCKS + m
                    dve.wait_ge(w4_done, j + 1)
                    xb = node_tiles(node_x, j * BT, BT)
                    nc.vector.tensor_tensor(xb, xb, psum[0:ROWS, m, :], ALU.add).then_inc(y_ready, 1)

        @block.tensor
        def _(pe):
            pe.wait_ge(weights_loaded, 16 * N_WEIGHTS)
            pe.wait_ge(consts_ready, 3)
            pe.wait_ge(ident_ready, 2)
            for layer in range(2):
                pe.sem_inc(summed[layer], RING)
            n_sweeps = sweeps(pe)

            def turn(q, i, r):
                k, rows = shape_of(i, r)
                g = q * N_CHUNKS + RING * number(i) + r
                pe.wait_ge(turned_copied, g)
                pe.wait_ge(onehot_ready[1], g + 1)
                oh = onehot[0:rows, r % 2, 0:k, :].bitcast(BF16)
                for t in range(k):
                    last = nc.tensor.transpose(ps_oht[0:WINDOW, t * rows:(t + 1) * rows],
                                               oh[:, t, 1:2 * WINDOW:2], ident_h[0:rows, 0:rows])
                last.then_inc(turned, 1)

            def products(layer, q, i, r):
                k, rows = shape_of(i, r)
                g = q * N_CHUNKS + RING * number(i) + r
                pe.wait_ge(mixed[layer], g)
                if layer == 0:
                    pe.wait_ge(feats_loaded[0][r], 16 * (q * GROUPS + number(i) + 1))
                else:
                    pe.wait_ge(turned_copied, g + 1)
                for t in range(k):
                    if layer == 0:
                        last = nc.tensor.matmul(ps_pre[0:rows, t, :], lhs[0:N_RBF, r, t * rows:(t + 1) * rows],
                                                w_rbf_s[:, :], start=True, stop=True)
                    else:
                        last = nc.tensor.matmul(ps_pre[0:rows, t, :], lhs[:, r, t * rows:(t + 1) * rows],
                                                win_b[:, r, :], start=True, stop=True)
                last.then_inc(products_ready[layer], 1)

            def sum_messages(layer, q, i, r):
                k, rows = shape_of(i, r)
                g = q * N_CHUNKS + RING * number(i) + r
                pe.wait_ge(sums_copied[layer], g)
                pe.wait_ge(onehot_ready[layer], g + 1)
                pe.wait_ge(messages_ready if layer else mixed[0], g + 1)
                for t in range(k):
                    last = nc.tensor.matmul(ps_sum, gath[0:rows, r, t, :], onehot[0:rows, r % 2, t, :],
                                            start=(t == 0), stop=(t == k - 1))
                if layer == 1:
                    oh = onehot[0:rows, r % 2, 0:k, :].bitcast(BF16)
                    for t in range(k):
                        last = nc.tensor.matmul(ps_deg, ones_h[0:rows, :], oh[:, t, 1:2 * WINDOW:2],
                                                 start=(t == 0), stop=(t == k - 1))
                last.then_inc(summed[layer], 1)

            def project(layer, q, i, r):
                g = q * N_CHUNKS + RING * number(i) + r
                pe.wait_ge(sums_copied[layer], g + 1)
                pe.wait_ge(acc_added[layer], g)
                if layer == 0:
                    nc.tensor.matmul(ps_proj, w1_s[:, :], sums[:, :], start=True, stop=True).then_inc(projected[0], 1)
                    return
                nc.tensor.matmul(ps_proj, m2_s[:, :], sums[:, :], start=True, stop=False)
                nc.tensor.matmul(ps_proj, mb2_s[:, :], deg[:, :], start=False, stop=True).then_inc(projected[1], 1)
                pe.wait_ge(projection_copied, g + 1)
                nc.tensor.matmul(ps_proj2, m3b_s[:, :], sums2[:, :], start=True, stop=True).then_inc(updated, 1)

            def edge_sweeps(layer):
                def step(q, i, r, nxt):
                    if nxt and layer:
                        turn(q, *nxt)
                    sum_messages(layer, q, i, r)
                    if nxt:
                        products(layer, q, *nxt)
                    project(layer, q, i, r)

                with pe.Fori(0, n_sweeps) as q:
                    if layer:
                        turn(q, 0, 0)
                    products(layer, q, 0, 0)
                    with pe.Fori(0, GROUPS - 2) as i:
                        for r in range(RING):
                            step(q, i, r, (i, r + 1) if r + 1 < RING else (i + 1, 0))
                    for r in range(RING):
                        step(q, GROUPS - 2, r, (GROUPS - 2, r + 1) if r + 1 < RING else (LAST, 0))
                    for r in range(RING):
                        step(q, LAST, r, (LAST, r + 1) if r + 1 < RING else None)

            edge_sweeps(0)

            def times_w2(j):
                pe.wait_ge(x2_ready, j)
                pe.wait_ge(u_ready, j + 1)
                for t in range(BT):
                    last = nc.tensor.matmul(ps_w[:, t * HID:(t + 1) * HID], u_buf[:, t * ROWS:(t + 1) * ROWS],
                                            w2_s[:, :], start=True, stop=True)
                last.then_inc(w2_done, 1)

            def turn_h(j):
                pe.wait_ge(ht_copied, j)
                pe.wait_ge(h2_ready, j + 1)
                for t in range(BT):
                    last = nc.tensor.transpose(ps_t[:, t * ROWS:(t + 1) * ROWS], h_buf[:, t * HID:(t + 1) * HID],
                                               ident[0:ROWS, 0:ROWS])
                last.then_inc(ht_ready, 1)

            def times_w1_w3(j):
                pe.wait_ge(ht_copied, j + 1)
                pe.wait_ge(b_ready, j)
                pe.wait_ge(c_ready, j)
                for t in range(BT):
                    nc.tensor.matmul(ps_ab[:, t, :], ht_buf[:, t * ROWS:(t + 1) * ROWS],
                                     m1ab_s[:, :, :].rearrange("p a f -> p (a f)"), start=True, stop=True)
                nc.tensor.matmul(ps_c, m3a_s[:, :], ht_buf, start=True, stop=True).then_inc(abc_done, 1)

            times_w2(0)
            times_w2(1)
            turn_h(0)
            with pe.Fori(2, BLOCKS) as j:
                times_w2(j)
                times_w1_w3(j - 2)
                turn_h(j - 1)
            times_w1_w3(BLOCKS - 2)
            turn_h(BLOCKS - 1)
            times_w1_w3(BLOCKS - 1)

            edge_sweeps(1)

            with pe.Fori(0, PIECES) as n:
                for m in range(PIECE_BLOCKS):
                    j = n * PIECE_BLOCKS + m
                    if m == 0:
                        pe.wait_ge(y_ready, j)
                    pe.wait_ge(v_ready, j + 1)
                    for t in range(BT):
                        v = lflat[:, m * BN + t * ROWS:m * BN + (t + 1) * ROWS]
                        last = nc.tensor.matmul(psum[0:ROWS, m, t * HID:(t + 1) * HID], v, m4_s[:, :],
                                                start=True, stop=True)
                    last.then_inc(w4_done, 1)


def kernel(**inputs):
    import concourse.bacc as _bacc
    from concourse.bass_utils import run_bass_kernel_spmd as _run

    a = {k: np.asarray(v) for k, v in inputs.items()}
    full = FULL * CHUNK

    def by_chunk(v):
        return v[:full].reshape(FULL * P, K), v[full:].reshape(TAIL_ROWS, TAIL_K)

    def features(v):
        n = v.shape[1]
        body = v[:full].reshape(FULL, P, K, n).transpose(0, 3, 2, 1).reshape(FULL * n, CHUNK)
        tail = v[full:].reshape(TAIL_ROWS, TAIL_K, n).transpose(2, 1, 0).reshape(n, TAIL)
        return body, tail

    (src, src_tail), (dst, dst_tail) = by_chunk(a["src"]), by_chunk(a["dst"])
    rbf, rbf_tail = features(a["edge_attr_6"])
    ef, ef_tail = features(a["edge_attr_16"])
    laid = {
        "x": a["x"], "dst": a["dst"],
        "ids": np.concatenate([src, dst], axis=1), "ids_tail": np.concatenate([src_tail, dst_tail], axis=1),
        "rbf": rbf, "rbf_tail": rbf_tail, "ef": ef, "ef_tail": ef_tail,
        "w_rbf_t": a["L0_gnn_W_rbf"].T, "w1_t": a["L0_gnn_W1"].T, "b1": a["L0_gnn_b1"][:, None],
        "w2_t": a["L0_gnn_W2"].T, "b2": a["L0_gnn_b2"][None, :],
        "m1": a["L1_gnn_W1"], "mb1": a["L1_gnn_b1"][None, :], "m2": a["L1_gnn_W2"], "mb2": a["L1_gnn_b2"][None, :],
        "m3": a["L1_gnn_W3"], "mb3": a["L1_gnn_b3"][:, None], "m4": a["L1_gnn_W4"], "mb4": a["L1_gnn_b4"][None, :],
    }
    nc = _bacc.Bacc("TRN2", target_bir_lowering=False, num_devices=1)
    arrays, args = {}, []
    for name, v in laid.items():
        v = np.ascontiguousarray(v)
        arrays[f"in_{name}"] = v
        args.append(nc.dram_tensor(f"in_{name}", v.shape, mybir.dt.from_np(v.dtype), kind="ExternalInput").ap())
    out = nc.dram_tensor("out_0", (N_NODES, HID), F32, kind="ExternalOutput").ap()
    gnn_kernel(nc, *args, out)
    r = _run(nc, [arrays], core_ids=[0])
    return r.results[0]["out_0"]
```

```python
from contextlib import ExitStack

import numpy as np
import concourse.bass as bass
from concourse import mybir

F32 = mybir.dt.float32
BF16 = mybir.dt.bfloat16
I32 = mybir.dt.int32
ALU = mybir.AluOpType
ACT = mybir.ActivationFunctionType
AX_X = mybir.AxisListType.X

N_NODES, N_EDGES, HID = 12500, 200000, 128
N_RBF, N_EF = 6, 16
LN_EPS = 1e-5
RSQRT_SEED, NEWTON = 0x5F3759DF, 4
P = 128
ROWS = 125
NODE_TILES = N_NODES // ROWS
BT = 4
SPLIT = ROWS // 16 * 16
BN = BT * ROWS
BLOCKS = NODE_TILES // BT
PIECES = 5
PIECE_TILES = NODE_TILES // PIECES
PIECE_BLOCKS = BLOCKS // PIECES
K = 8
CHUNK = K * P
FULL = N_EDGES // CHUNK
TAIL = N_EDGES - FULL * CHUNK
TAIL_K = 4
TAIL_ROWS = TAIL // TAIL_K
N_CHUNKS = FULL + 1
RING = 4
GROUPS = N_CHUNKS // RING
WINDOW = P - N_EF
MIN_P = FULL // 3
assert TAIL_K * TAIL_ROWS == TAIL and GROUPS * RING == N_CHUNKS and MIN_P * 3 == FULL


def gnn_kernel(nc, x, dst, ids, ids_tail, rbf, rbf_tail, ef, ef_tail, w_rbf_t, w1_t, b1, w2_t, b2,
               m1, mb1, m2, mb2, m3, mb3, m4, mb4, out):
    h_table = nc.dram_tensor("h_table", (N_NODES, HID), F32).ap()
    a_table = nc.dram_tensor("a_table", (N_NODES, HID), F32).ap()
    b_table = nc.dram_tensor("b_table", (N_NODES + WINDOW, HID), F32).ap()
    lo_table = nc.dram_tensor("lo_table", (1, N_CHUNKS), F32).ap()
    hi_table = nc.dram_tensor("hi_table", (1, N_CHUNKS), F32).ap()

    with ExitStack() as ctx:
        def sb(name, shape, dt=F32):
            return ctx.enter_context(nc.sbuf_tensor(name, shape, dt))

        def sem(name):
            return ctx.enter_context(nc.semaphore(name))

        def sems(name, n):
            return [sem(f"{name}{i}") for i in range(n)]

        acc = sb("acc", [P, N_NODES + WINDOW])
        node_x = sb("node_x", [ROWS, NODE_TILES * HID])
        node_h = sb("node_h", [ROWS, NODE_TILES * HID])
        gath = sb("gath", [P, RING, K, HID])
        lhs = sb("lhs", [P, RING, CHUNK])
        onehot = sb("onehot", [P, 2, K, WINDOW])
        win_b = sb("win_b", [P, RING, HID])
        idst = sb("idst", [P, RING, 2 * K], I32)
        rel = sb("rel", [P, 2, K])
        iota_w = sb("iota_w", [P, WINDOW])
        chunk_lo = sb("chunk_lo", [P, N_CHUNKS])
        win_lo = sb("win_lo", [P, N_CHUNKS])
        base_i = sb("base_i", [1, N_CHUNKS], I32)
        hi_row = sb("hi_row", [1, N_CHUNKS])
        lo3 = sb("lo3", [MIN_P, 3])
        hi3 = sb("hi3", [MIN_P, 3])
        lo_t = sb("lo_t", [1, 1])
        hi_t = sb("hi_t", [1, 1])
        span = sb("span", [1, N_CHUNKS])
        span_max = sb("span_max", [1, 1])
        span_i = sb("span_i", [1, 1], I32)
        sums = sb("sums", [P, WINDOW])
        sums2 = sb("sums2", [P, WINDOW])
        deg = sb("deg", [1, WINDOW])
        ident = sb("ident", [P, P])
        ident_h = sb("ident_h", [P, P], BF16)
        ones_h = sb("ones_h", [P, 1], BF16)
        stats = sb("stats", [ROWS, NODE_TILES, 6])
        rstd = sb("rstd", [ROWS, NODE_TILES])
        nmr = sb("nmr", [ROWS, NODE_TILES])
        w_rbf_s = sb("w_rbf_s", [N_RBF, HID])
        w1_s = sb("w1_s", [P, HID])
        w2_s = sb("w2_s", [P, HID])
        m1ab_s = sb("m1ab_s", [P, 2, HID])
        m2_s = sb("m2_s", [P, HID])
        m3a_s = sb("m3a_s", [P, HID])
        m3b_s = sb("m3b_s", [P, HID])
        m4_s = sb("m4_s", [P, HID])
        b1_s = sb("b1_s", [P, 1])
        mb3_s = sb("mb3_s", [P, 1])
        b2_s = sb("b2_s", [ROWS, HID])
        mb1_s = sb("mb1_s", [ROWS, HID])
        mb4_s = sb("mb4_s", [ROWS, HID])
        mb2_s = sb("mb2_s", [1, HID])
        psum = ctx.enter_context(nc.psum_tensor("psum", [P, 8, 512], F32))

        gflat = gath[:, :, :, :].rearrange("p r k f -> p (r k f)")
        dst3 = gflat[0:MIN_P, 0:3 * CHUNK].bitcast(I32).rearrange("p (k e) -> p k e", k=3)
        dst_t = gflat[0:1, 3 * CHUNK:3 * CHUNK + TAIL].bitcast(I32)
        lflat = lhs[:, :, :].rearrange("p r e -> p (r e)")
        u_buf = [lflat[:, m * BN:(m + 1) * BN] for m in range(PIECE_BLOCKS)]
        ht_buf = [lflat[:, m * BN:(m + 1) * BN] for m in range(2)]
        h_buf = lflat[0:ROWS, 2 * CHUNK:2 * CHUNK + BT * HID]
        half_sum, diff, squares, neg_mean, var_eps, newton, seed_f = (
            lflat[0:ROWS, 3 * CHUNK + n * NODE_TILES:3 * CHUNK + (n + 1) * NODE_TILES] for n in range(7))
        seed = seed_f.bitcast(I32)
        b_stage = gflat[0:ROWS, 0:BT * HID]
        zeros = onehot[:, :, :, :].rearrange("p a k w -> p (a k w)")[0:WINDOW, 0:HID]
        ps_pre = psum[:, 0:2, :].rearrange("p a (k f) -> p (a k) f", f=HID)
        ps_oht = psum[:, 2, :].bitcast(BF16)
        ps_sum = psum[:, 3, 0:WINDOW]
        ps_deg = psum[0:1, 3, 256:256 + WINDOW]
        ps_proj = psum[:, 4, 0:WINDOW]
        ps_proj2 = psum[:, 5, 0:WINDOW]
        ps_t = psum[:, 0, 0:BN]
        ps_c = psum[:, 1, 0:BN]
        ps_ab = psum[0:ROWS, 2:4, :].rearrange("p a (k f) -> p (a k) f", f=2 * HID)

        def node_tiles(ap, j0, n):
            return ap[:, bass.ds(j0 * HID, n * HID)]

        def table_rows(t, j0, n):
            return t[bass.ds(j0 * ROWS, n * ROWS), :].rearrange("(j p) f -> p j f", p=ROWS)

        waited = {name: sem(f"waited_{name}") for name in ("dve", "pool", "sp")}
        x_loaded = sems("x_loaded", PIECES)
        dst_loaded = sem("dst_loaded")
        weights_loaded = sem("weights_loaded")
        extremes_ready = sem("extremes_ready")
        extremes_stored = sem("extremes_stored")
        extremes_loaded = sem("extremes_loaded")
        span_steps = sem("span_steps")
        span_ready = sem("span_ready")
        consts_ready = sem("consts_ready")
        ident_zero = sem("ident_zero")
        ident_ready = sem("ident_ready")
        acc_zeroed = sem("acc_zeroed")
        zeros_ready = sem("zeros_ready")
        zeros_stored = sem("zeros_stored")
        stats_step = sem("stats_step")
        norm_ready = sem("norm_ready")
        h_ready = sem("h_ready")
        h_stored = sem("h_stored")
        bias_added = sem("bias_added")
        summed = sems("summed", 2)
        ids_loaded = [sems(f"ids_loaded{l}_", RING) for l in range(2)]
        feats_loaded = [sems(f"feats_loaded{l}_", RING) for l in range(2)]
        gathered = [sems(f"gathered{l}_", RING) for l in range(2)]
        window_step = sems("window_step", 2)
        window_ready = sems("window_ready", 2)
        rel_ready = sems("rel_ready", 2)
        onehot_ready = sems("onehot_ready", 2)
        turned = sem("turned")
        turned_copied = sem("turned_copied")
        products_ready = sems("products_ready", 2)
        mixed = sems("mixed", 2)
        messages_ready = sem("messages_ready")
        sums_copied = sems("sums_copied", 2)
        projected = sems("projected", 2)
        projection_copied = sem("projection_copied")
        updated = sem("updated")
        acc_added = sems("acc_added", 2)
        u_ready = sem("u_ready")
        w2_done = sem("w2_done")
        x2_ready = sem("x2_ready")
        stats2_step = sem("stats2_step")
        norm2_ready = sem("norm2_ready")
        h2_ready = sem("h2_ready")
        xh_ready = sem("xh_ready")
        ht_ready = sem("ht_ready")
        ht_copied = sem("ht_copied")
        ab_done = sem("ab_done")
        c_done = sem("c_done")
        a_ready = sem("a_ready")
        b_ready = sem("b_ready")
        c_ready = sem("c_ready")
        a_stored = sem("a_stored")
        b_stored = sem("b_stored")
        b_taken = sem("b_taken")
        v_ready = sem("v_ready")
        w4_done = sem("w4_done")
        y_ready = sem("y_ready")
        out_stored = sem("out_stored")

        N_WEIGHTS = 15 + RING
        from_one = [*mixed, *acc_added, *sums_copied, turned_copied, w2_done, x2_ready, ht_ready, ht_copied,
                    xh_ready, b_ready, c_ready, b_taken, w4_done, y_ready]

        def done(n):
            return n + 1

        def sweeps(eng):
            eng.wait_ge(span_ready, 1)
            widest = eng.value_load(span_i[0:1, 0:1], min_val=0, max_val=N_NODES - 1)
            return widest // WINDOW + 1

        def shape_of(i, r):
            return (TAIL_K, TAIL_ROWS) if i is LAST and r == RING - 1 else (K, P)

        LAST = "last"

        def number(i):
            return GROUPS - 1 if i is LAST else i

        def following(i, r):
            if r + 1 < RING:
                return i, r + 1
            return None if i is LAST else (i + 1, 0)

        def gathered_count(q, i, r):
            per_sweep = 16 * (K * (GROUPS - 1) + shape_of(LAST, r)[0])
            return q * per_sweep + 16 * K * number(i) + 16 * shape_of(i, r)[0]

        block = ctx.enter_context(nc.Block())

        @block.sync
        def _(sp):
            def load_nodes(tile, table, j0, n, done):
                dram = table_rows(table, j0, n)
                on_chip = tile.rearrange("p (j f) -> p j f", f=HID)
                for lo, hi in ((0, SPLIT), (SPLIT, ROWS)):
                    sp.dma_start(on_chip[lo:hi], dram[lo:hi]).then_inc(done, 16)

            def store_nodes(table, j0, n, tile, done):
                dram = table_rows(table, j0, n)
                on_chip = tile.rearrange("p (j f) -> p j f", f=HID)
                for lo, hi in ((0, SPLIT), (SPLIT, ROWS)):
                    sp.dma_start(dram[lo:hi], on_chip[lo:hi]).then_inc(done, 16)

            sp.dma_start(dst3, dst[0:FULL * CHUNK].rearrange("(p k e) -> p k e", k=3, e=CHUNK)
                         ).then_inc(dst_loaded, 16)
            sp.dma_start(dst_t, dst[FULL * CHUNK:N_EDGES].rearrange("(a e) -> a e", a=1)).then_inc(dst_loaded, 16)
            for n in range(PIECES):
                load_nodes(node_tiles(node_x, n * PIECE_TILES, PIECE_TILES), x, n * PIECE_TILES, PIECE_TILES,
                           x_loaded[n])
            for tile, src in ((w_rbf_s[:, :], w_rbf_t), (w1_s[:, :], w1_t), (w2_s[:, :], w2_t),
                              (m1ab_s[:, 0, :], m1[0:HID, :]), (m1ab_s[:, 1, :], m1[HID:2 * HID, :]),
                              (m2_s[:, :], m2), (m3a_s[:, :], m3[0:HID, :]), (m3b_s[:, :], m3[HID:2 * HID, :]),
                              (m4_s[:, :], m4), (b1_s[:, :], b1), (mb3_s[:, :], mb3), (mb2_s[:, :], mb2),
                              (b2_s[:, :], b2.partition_broadcast(ROWS)), (mb1_s[:, :], mb1.partition_broadcast(ROWS)),
                              (mb4_s[:, :], mb4.partition_broadcast(ROWS))):
                sp.dma_start(tile, src).then_inc(weights_loaded, 16)
            for r in range(RING):
                sp.dma_start(win_b[WINDOW:P, r, :], m1[2 * HID:2 * HID + N_EF, :]).then_inc(weights_loaded, 16)
            sp.wait_ge(extremes_ready, 4)
            sp.dma_start(lo_table[0, 0:FULL].rearrange("(p k) -> p k", k=3), lo3[:, :]).then_inc(extremes_stored, 16)
            sp.dma_start(hi_table[0, 0:FULL].rearrange("(p k) -> p k", k=3), hi3[:, :]).then_inc(extremes_stored, 16)
            sp.dma_start(lo_table[:, FULL:N_CHUNKS], lo_t[:, :]).then_inc(extremes_stored, 16)
            sp.dma_start(hi_table[:, FULL:N_CHUNKS], hi_t[:, :]).then_inc(extremes_stored, 16)
            sp.wait_ge(extremes_stored, 64)
            sp.dma_start(chunk_lo[:, :], lo_table.partition_broadcast(P)).then_inc(extremes_loaded, 16)
            sp.dma_start(hi_row[:, :], hi_table).then_inc(extremes_loaded, 16)
            sp.wait_ge(zeros_ready, 1)
            sp.dma_start(b_table[N_NODES:N_NODES + WINDOW, :], zeros).then_inc(zeros_stored, 16)
            for n in range(PIECES):
                sp.wait_ge(h_ready, PIECE_BLOCKS * (n + 1))
                store_nodes(h_table, n * PIECE_TILES, PIECE_TILES, node_tiles(node_h, n * PIECE_TILES, PIECE_TILES),
                            h_stored)

            n_sweeps = sweeps(sp)

            def load_group(layer, q, i):
                for r in range(RING):
                    k, rows = shape_of(i, r)
                    c = RING * number(i) + r
                    sp.wait_ge(summed[layer], q * N_CHUNKS + c + 1)
                    tail = k != K
                    ids_src = ids_tail if tail else ids[bass.ds(c * P, P), :]
                    sp.dma_start(idst[0:rows, r, 0:2 * k], ids_src).then_inc(ids_loaded[layer][r], 16)
                    if layer == 0:
                        src = rbf_tail if tail else rbf[bass.ds(c * N_RBF, N_RBF), :]
                        sp.dma_start(lhs[0:N_RBF, r, 0:k * rows], src).then_inc(feats_loaded[0][r], 16)
                    else:
                        src = ef_tail if tail else ef[bass.ds(c * N_EF, N_EF), :]
                        sp.dma_start(lhs[WINDOW:P, r, 0:k * rows], src).then_inc(feats_loaded[1][r], 16)
                        base = sp.value_load(base_i[0:1, bass.ds(c, 1)], min_val=0, max_val=N_NODES)
                        sp.dma_start(win_b[0:WINDOW, r, :], b_table[bass.ds(base, WINDOW), :]
                                     ).then_inc(feats_loaded[1][r], 16)

            with sp.Fori(0, n_sweeps) as q:
                with sp.Fori(0, GROUPS - 1) as i:
                    load_group(0, q, i)
                load_group(0, q, LAST)

            def store_ab(j):
                sp.wait_ge(a_ready, j + 1)
                store_nodes(a_table, j * BT, BT, node_tiles(node_h, j * BT, BT), a_stored)
                sp.wait_ge(b_ready, done(j + 1))
                store_nodes(b_table, j * BT, BT, b_stage, b_stored)
                sp.wait_ge(b_stored, 32 * (j + 1))
                sp.sem_inc(b_taken, 1)

            with sp.Fori(0, BLOCKS) as j:
                store_ab(j)
            sp.wait_ge(b_stored, 32 * BLOCKS)
            sp.wait_ge(a_stored, 32 * BLOCKS)
            sp.wait_ge(zeros_stored, 16)

            with sp.Fori(0, n_sweeps) as q:
                sp.wait_ge(window_ready[1], q + 1)
                sp.sem_inc(waited["sp"], 1)
                with sp.Fori(0, GROUPS - 1) as i:
                    load_group(1, q, i)
                load_group(1, q, LAST)

            for n in range(PIECES):
                sp.wait_ge(y_ready, done(PIECE_BLOCKS * (n + 1)))
                store_nodes(out, n * PIECE_TILES, PIECE_TILES, node_tiles(node_x, n * PIECE_TILES, PIECE_TILES),
                            out_stored)
            sp.wait_ge(out_stored, 32 * PIECES)
            sp.wait_ge(h_stored, 32 * PIECES)
            sp.wait_ge(weights_loaded, 16 * N_WEIGHTS)

        @block.gpsimd
        def _(pool):
            nc.gpsimd.iota(iota_w[:, :], pattern=[[1, WINDOW]], base=0, channel_multiplier=0,
                           allow_small_or_imprecise_dtypes=True).then_inc(consts_ready, 1)
            nc.gpsimd.memset(ones_h[:, :], 1.0).then_inc(consts_ready, 1)
            nc.gpsimd.memset(ident[:, :], 0.0).then_inc(ident_zero, 1)
            nc.gpsimd.memset(ident_h[:, :], 0.0).then_inc(ident_zero, 1)
            nc.gpsimd.memset(zeros, 0.0).then_inc(zeros_ready, 1)
            pool.wait_ge(ident_zero, 2)
            nc.gpsimd.affine_select(out=ident[:, :], in_=ident[:, :], compare_op=ALU.not_equal, fill=1.0,
                                    base=0, pattern=[[-1, P]], channel_multiplier=1).then_inc(ident_ready, 1)
            nc.gpsimd.affine_select(out=ident_h[:, :], in_=ident_h[:, :], compare_op=ALU.not_equal, fill=1.0,
                                    base=0, pattern=[[-1, P]], channel_multiplier=1).then_inc(ident_ready, 1)

            nc.gpsimd.memset(acc[:, :], 0.0).then_inc(acc_zeroed, 1)

            n_sweeps = sweeps(pool)

            def gather_group(layer, table, q, i):
                for r in range(RING):
                    k, rows = shape_of(i, r)
                    pool.wait_ge(ids_loaded[layer][r], 16 * (q * GROUPS + number(i) + 1))
                    pool.sem_inc(waited["pool"], 1)
                    for t in range(k):
                        pool.indirect_dma_start(
                            out=gath[0:rows, r, t, :], out_offset=None, in_=table,
                            in_offset=bass.IndirectOffsetOnAxis(ap=idst[0:rows, r, t:t + 1], axis=0),
                        ).then_inc(gathered[layer][r], 16)

            pool.wait_ge(h_stored, 32 * PIECES)
            with pool.Fori(0, n_sweeps) as q:
                with pool.Fori(0, GROUPS - 1) as i:
                    gather_group(0, h_table, q, i)
                gather_group(0, h_table, q, LAST)

            def residual(j):
                pool.wait_ge(h2_ready, j + 1)
                pool.sem_inc(waited["pool"], 1)
                xb = node_tiles(node_x, j * BT, BT)
                nc.gpsimd.tensor_tensor(xb, xb, h_buf, ALU.add).then_inc(xh_ready, 1)

            with pool.Fori(0, BLOCKS) as j:
                residual(j)

            pool.wait_ge(a_stored, 32 * BLOCKS)
            with pool.Fori(0, n_sweeps) as q:
                with pool.Fori(0, GROUPS - 1) as i:
                    gather_group(1, a_table, q, i)
                gather_group(1, a_table, q, LAST)

        @block.scalar
        def _(act):
            for s in from_one:
                act.sem_inc(s, 1)

            def normalise(j, into, ready):
                for t in range(BT):
                    col = bass.ds(j * BT + t, 1)
                    last = nc.scalar.activation(into(t), node_tiles(node_x, j * BT + t, 1), ACT.Relu,
                                                bias=nmr[:, col], scale=rstd[:, col])
                last.then_inc(ready, 1)

            for n in range(PIECES):
                act.wait_ge(norm_ready, n + 1)
                with act.Fori(n * PIECE_BLOCKS, (n + 1) * PIECE_BLOCKS) as j:
                    normalise(j, lambda t: node_tiles(node_h, j * BT + t, 1), h_ready)

            n_sweeps = sweeps(act)

            def copy_sums(layer, g):
                act.wait_ge(summed[layer], RING + g + 1)
                if layer == 1:
                    nc.scalar.copy(deg[:, :], ps_deg)
                nc.scalar.copy(sums[:, :], ps_sum).then_inc(sums_copied[layer], 1)

            with act.Fori(0, n_sweeps) as q:
                with act.Fori(0, N_CHUNKS) as c:
                    copy_sums(0, q * N_CHUNKS + c)

            def silu_piece(n, bias, used, ready):
                for m in range(PIECE_BLOCKS):
                    j = n * PIECE_BLOCKS + m
                    if m == 0:
                        act.wait_ge(used, done(j))
                    nc.scalar.activation(u_buf[m], acc[:, bass.ds(j * BN, BN)], ACT.Silu, **bias).then_inc(ready, 1)

            act.wait_ge(acc_added[0], done(n_sweeps * N_CHUNKS))
            act.wait_ge(weights_loaded, 16 * N_WEIGHTS)
            with act.Fori(0, PIECES) as n:
                silu_piece(n, {"bias": b1_s[:, 0:1]}, w2_done, u_ready)

            def normalise2(j):
                act.wait_ge(ht_ready, done(j))
                act.wait_ge(xh_ready, done(j))
                normalise(j, lambda t: h_buf[:, t * HID:(t + 1) * HID], h2_ready)

            def copy_ht(j, m):
                act.wait_ge(ht_ready, done(j + 1))
                nc.scalar.copy(ht_buf[m], ps_t).then_inc(ht_copied, 1)

            def keep_c(j):
                act.wait_ge(c_done, j + 1)
                nc.scalar.activation(acc[:, bass.ds(j * BN, BN)], ps_c, ACT.Identity, bias=mb3_s[:, 0:1]
                                     ).then_inc(c_ready, 1)

            act.wait_ge(norm2_ready, 1)
            normalise2(0)
            copy_ht(0, 0)
            normalise2(1)
            with act.Fori(0, BLOCKS // 2 - 1) as i:
                for m in range(2):
                    j = 2 * i + m
                    copy_ht(j + 1, 1 - m)
                    normalise2(j + 2)
                    keep_c(j)
            copy_ht(BLOCKS - 2, 1)
            normalise2(BLOCKS - 1)
            keep_c(BLOCKS - 3)
            copy_ht(BLOCKS - 1, 0)
            keep_c(BLOCKS - 2)
            keep_c(BLOCKS - 1)

            def copy_turned(q, i, r):
                k, rows = shape_of(i, r)
                g = q * N_CHUNKS + RING * number(i) + r
                act.wait_ge(feats_loaded[1][r], 32 * (q * GROUPS + number(i) + 1))
                act.wait_ge(turned, g + 1)
                nc.scalar.copy(lhs[0:WINDOW, r, 0:k * rows], ps_oht[0:WINDOW, 0:k * rows]).then_inc(turned_copied, 1)

            def silu_messages(q, i, r):
                k, rows = shape_of(i, r)
                act.wait_ge(mixed[1], done(q * N_CHUNKS + RING * number(i) + r + 1))
                nc.scalar.activation(gath[0:rows, r, 0:k, :], gath[0:rows, r, 0:k, :], ACT.Silu
                                     ).then_inc(messages_ready, 1)

            def copy_projection(g):
                act.wait_ge(projected[1], g + 1)
                nc.scalar.copy(sums2[:, :], ps_proj).then_inc(projection_copied, 1)

            def step(q, i, r, first=False):
                g = q * N_CHUNKS + RING * number(i) + r
                if not first:
                    copy_projection(g - 1)
                silu_messages(q, i, r)
                if following(i, r):
                    copy_turned(q, *following(i, r))
                copy_sums(1, g)

            with act.Fori(0, n_sweeps) as q:
                copy_turned(q, 0, 0)
                for r in range(RING):
                    step(q, 0, r, first=(r == 0))
                with act.Fori(1, GROUPS - 1) as i:
                    for r in range(RING):
                        step(q, i, r)
                for r in range(RING):
                    step(q, LAST, r)
                copy_projection((q + 1) * N_CHUNKS - 1)

            act.wait_ge(acc_added[1], done(n_sweeps * N_CHUNKS))
            with act.Fori(0, PIECES) as n:
                silu_piece(n, {}, w4_done, v_ready)

        @block.vector
        def _(dve):
            dve.wait_ge(dst_loaded, 32)
            nc.vector.tensor_reduce(lo3[:, :], dst3, AX_X, ALU.min).then_inc(extremes_ready, 1)
            nc.vector.tensor_reduce(hi3[:, :], dst3, AX_X, ALU.max).then_inc(extremes_ready, 1)
            nc.vector.tensor_reduce(lo_t[:, :], dst_t, AX_X, ALU.min).then_inc(extremes_ready, 1)
            nc.vector.tensor_reduce(hi_t[:, :], dst_t, AX_X, ALU.max).then_inc(extremes_ready, 1)

            def tile_stats(j):
                for t in range(BT):
                    last = nc.vector.bn_stats(stats[:, bass.ds(j * BT + t, 1), :].rearrange("p a b -> p (a b)"),
                                              node_tiles(node_x, j * BT + t, 1))
                return last

            def rstd_of(lo, hi, step, before, ready):
                count = [before]

                def after(*instructions):
                    for ins in instructions:
                        ins.then_inc(step, 1)
                    count[0] += len(instructions)
                    dve.wait_ge(step, count[0])

                mean_e, sq_e = stats[:, lo:hi, 1], stats[:, lo:hi, 2]
                mean_o, sq_o = stats[:, lo:hi, 4], stats[:, lo:hi, 5]
                hs, df, sq, nm = half_sum[:, lo:hi], diff[:, lo:hi], squares[:, lo:hi], neg_mean[:, lo:hi]
                ve, y, t = var_eps[:, lo:hi], rstd[:, lo:hi], newton[:, lo:hi]
                after(nc.vector.tensor_scalar(hs, mean_o, -0.5, None, ALU.mult),
                      nc.vector.tensor_tensor(df, mean_e, mean_o, ALU.subtract),
                      nc.vector.tensor_tensor(sq, sq_e, sq_o, ALU.add))
                after(nc.vector.scalar_tensor_tensor(out=nm, in0=mean_e, scalar=-0.5, in1=hs,
                                                     op0=ALU.mult, op1=ALU.add),
                      nc.vector.scalar_tensor_tensor(out=ve, in0=df, scalar=0.25, in1=df,
                                                     op0=ALU.mult, op1=ALU.mult),
                      nc.vector.tensor_scalar(sq, sq, 1.0 / HID, LN_EPS, ALU.mult, ALU.add))
                after(nc.vector.tensor_tensor(ve, ve, sq, ALU.add))
                after(nc.vector.tensor_scalar(seed[:, lo:hi], ve.bitcast(I32), 1, None, ALU.logical_shift_right))
                after(nc.vector.tensor_scalar(y.bitcast(I32), seed[:, lo:hi], -1, RSQRT_SEED, ALU.mult, ALU.add))
                for _ in range(NEWTON):
                    after(nc.vector.tensor_tensor(t, y, y, ALU.mult))
                    after(nc.vector.scalar_tensor_tensor(out=t, in0=t, scalar=-0.5, in1=ve,
                                                         op0=ALU.mult, op1=ALU.mult))
                    after(nc.vector.scalar_tensor_tensor(out=y, in0=t, scalar=1.5, in1=y,
                                                         op0=ALU.add, op1=ALU.mult))
                nc.vector.tensor_tensor(nmr[:, lo:hi], nm, y, ALU.mult).then_inc(ready, 1)
                return count[0]

            steps = 0
            for n in range(PIECES):
                dve.wait_ge(x_loaded[n], 32)
                with dve.Fori(n * PIECE_BLOCKS, (n + 1) * PIECE_BLOCKS) as j:
                    tile_stats(j).then_inc(stats_step, 1)
                steps += PIECE_BLOCKS
                dve.wait_ge(stats_step, steps)
                steps = rstd_of(n * PIECE_TILES, (n + 1) * PIECE_TILES, stats_step, steps, norm_ready)

            dve.wait_ge(extremes_loaded, 32)
            nc.vector.tensor_tensor(span[:, :], hi_row[:, :], chunk_lo[0:1, :], ALU.subtract).then_inc(span_steps, 1)
            dve.wait_ge(span_steps, 1)
            nc.vector.tensor_reduce(span_max[:, :], span[:, :], AX_X, ALU.max).then_inc(span_steps, 1)
            dve.wait_ge(span_steps, 2)
            nc.vector.tensor_copy(span_i[:, :], span_max[:, :]).then_inc(span_ready, 1)

            dve.wait_ge(weights_loaded, 16 * N_WEIGHTS)
            for n in range(PIECES):
                dve.wait_ge(h_ready, PIECE_BLOCKS * (n + 1))
                xv = node_tiles(node_x, n * PIECE_TILES, PIECE_TILES).rearrange("p (j f) -> p j f", f=HID)
                nc.vector.tensor_tensor(xv, xv, b2_s[:, :].unsqueeze(1).broadcast_to([ROWS, PIECE_TILES, HID]),
                                        ALU.add).then_inc(bias_added, 1)

            n_sweeps = sweeps(dve)

            def base_row(layer):
                nc.vector.tensor_scalar(base_i[:, :], win_lo[0:1, :], float(N_NODES), None, ALU.min
                                        ).then_inc(window_ready[layer], 1)

            def build_onehot(layer, q, i, r, chunks_summed):
                k, rows = shape_of(i, r)
                c = RING * number(i) + r
                dve.wait_ge(ids_loaded[layer][r], 16 * (q * GROUPS + number(i) + 1))
                nc.vector.tensor_scalar(rel[0:rows, r % 2, 0:k], idst[0:rows, r, k:2 * k],
                                        win_lo[0:rows, bass.ds(c, 1)], None, ALU.subtract).then_inc(rel_ready[layer], 1)
                dve.wait_ge(summed[layer], RING + chunks_summed)
                dve.wait_ge(rel_ready[layer], q * N_CHUNKS + c + 1)
                nc.vector.tensor_tensor(onehot[0:rows, r % 2, 0:k, :],
                                        rel[0:rows, r % 2, 0:k].unsqueeze(2).broadcast_to([rows, k, WINDOW]),
                                        iota_w[0:rows, :].unsqueeze(1).broadcast_to([rows, k, WINDOW]),
                                        ALU.is_equal).then_inc(onehot_ready[layer], 1)

            def mix(layer, q, i, r):
                k, rows = shape_of(i, r)
                g = q * N_CHUNKS + RING * number(i) + r
                dve.wait_ge(products_ready[layer], g + 1)
                dve.wait_ge(gathered[layer][r], gathered_count(q, i, r))
                gv = gath[0:rows, r, 0:k, :]
                nc.vector.tensor_tensor(gv, gv, ps_pre[0:rows, 0:k, :], ALU.add if layer else ALU.mult
                                        ).then_inc(mixed[layer], 1)

            def add_window(layer, q, c):
                g = q * N_CHUNKS + c
                base = dve.value_load(base_i[0:1, bass.ds(c, 1)], min_val=0, max_val=N_NODES)
                dve.wait_ge(updated if layer else projected[0], g + 1)
                dve.wait_ge(acc_added[layer], done(g))
                av = acc[:, bass.ds(base, WINDOW)]
                nc.vector.tensor_tensor(av, av, ps_proj2 if layer else ps_proj, ALU.add
                                        ).then_inc(acc_added[layer], 1)

            def edge_sweeps(layer):
                nc.vector.tensor_copy(win_lo[:, :], chunk_lo[:, :]).then_inc(window_step[layer], 1)
                dve.wait_ge(window_step[layer], 1)
                base_row(layer)

                def step(q, i, r, first=False):
                    c = RING * number(i) + r
                    mix(layer, q, i, r)
                    if following(i, r):
                        build_onehot(layer, q, *following(i, r), q * N_CHUNKS + c)
                    if not first:
                        add_window(layer, q, c - 1)

                with dve.Fori(0, n_sweeps) as q:
                    dve.wait_ge(window_ready[layer], q + 1)
                    build_onehot(layer, q, 0, 0, q * N_CHUNKS)
                    for r in range(RING):
                        step(q, 0, r, first=(r == 0))
                    with dve.Fori(1, GROUPS - 1) as i:
                        for r in range(RING):
                            step(q, i, r)
                    for r in range(RING):
                        step(q, LAST, r)
                    add_window(layer, q, N_CHUNKS - 1)
                    dve.wait_ge(acc_added[layer], done((q + 1) * N_CHUNKS))
                    nc.vector.tensor_scalar(win_lo[:, :], win_lo[:, :], float(WINDOW), None, ALU.add
                                            ).then_inc(window_step[layer], 1)
                    dve.wait_ge(window_step[layer], q + 2)
                    base_row(layer)

            dve.wait_ge(consts_ready, 2)
            dve.wait_ge(acc_zeroed, 1)
            dve.wait_ge(zeros_stored, 16)
            edge_sweeps(0)

            dve.wait_ge(bias_added, PIECES)
            with dve.Fori(0, PIECES) as n:
                for m in range(PIECE_BLOCKS):
                    j = n * PIECE_BLOCKS + m
                    dve.wait_ge(w2_done, done(j + 1))
                    xb = node_tiles(node_x, j * BT, BT)
                    nc.vector.tensor_tensor(xb, xb, psum[0:ROWS, m, :], ALU.add).then_inc(x2_ready, 1)
                    dve.wait_ge(x2_ready, done(j + 1))
                    dve.sem_inc(waited["dve"], 1)
                    tile_stats(j).then_inc(stats2_step, 1)
            dve.wait_ge(stats2_step, BLOCKS)
            rstd_of(0, NODE_TILES, stats2_step, BLOCKS, norm2_ready)

            with dve.Fori(0, BLOCKS) as j:
                dve.wait_ge(ab_done, j + 1)
                nc.vector.tensor_copy(node_tiles(node_h, j * BT, BT).rearrange("p (j f) -> p j f", f=HID),
                                      ps_ab[:, :, 0:HID]).then_inc(a_ready, 1)
                dve.wait_ge(b_taken, done(j))
                nc.vector.tensor_tensor(b_stage.rearrange("p (j f) -> p j f", f=HID), ps_ab[:, :, HID:2 * HID],
                                        mb1_s[:, :].unsqueeze(1).broadcast_to([ROWS, BT, HID]), ALU.add
                                        ).then_inc(b_ready, 1)

            dve.wait_ge(c_ready, done(BLOCKS))
            dve.wait_ge(xh_ready, done(BLOCKS))
            for n in range(PIECES):
                xv = node_tiles(node_x, n * PIECE_TILES, PIECE_TILES).rearrange("p (j f) -> p j f", f=HID)
                nc.vector.tensor_tensor(xv, xv, mb4_s[:, :].unsqueeze(1).broadcast_to([ROWS, PIECE_TILES, HID]),
                                        ALU.add).then_inc(bias_added, 1)
            dve.wait_ge(bias_added, 2 * PIECES)
            edge_sweeps(1)

            with dve.Fori(0, PIECES) as n:
                for m in range(PIECE_BLOCKS):
                    j = n * PIECE_BLOCKS + m
                    dve.wait_ge(w4_done, done(j + 1))
                    xb = node_tiles(node_x, j * BT, BT)
                    nc.vector.tensor_tensor(xb, xb, psum[0:ROWS, m, :], ALU.add).then_inc(y_ready, 1)

        @block.tensor
        def _(pe):
            pe.wait_ge(weights_loaded, 16 * N_WEIGHTS)
            pe.wait_ge(consts_ready, 2)
            pe.wait_ge(ident_ready, 2)
            for layer in range(2):
                pe.sem_inc(summed[layer], RING)
            n_sweeps = sweeps(pe)

            def turn(q, i, r):
                k, rows = shape_of(i, r)
                g = q * N_CHUNKS + RING * number(i) + r
                pe.wait_ge(turned_copied, done(g))
                pe.wait_ge(onehot_ready[1], g + 1)
                oh = onehot[0:rows, r % 2, 0:k, :].bitcast(BF16)
                for t in range(k):
                    last = nc.tensor.transpose(ps_oht[0:WINDOW, t * rows:(t + 1) * rows],
                                               oh[:, t, 1:2 * WINDOW:2], ident_h[0:rows, 0:rows])
                last.then_inc(turned, 1)

            def products(layer, q, i, r):
                k, rows = shape_of(i, r)
                g = q * N_CHUNKS + RING * number(i) + r
                pe.wait_ge(mixed[layer], done(g))
                if layer == 0:
                    pe.wait_ge(feats_loaded[0][r], 16 * (q * GROUPS + number(i) + 1))
                else:
                    pe.wait_ge(turned_copied, done(g + 1))
                for t in range(k):
                    if layer == 0:
                        last = nc.tensor.matmul(ps_pre[0:rows, t, :], lhs[0:N_RBF, r, t * rows:(t + 1) * rows],
                                                w_rbf_s[:, :], start=True, stop=True)
                    else:
                        last = nc.tensor.matmul(ps_pre[0:rows, t, :], lhs[:, r, t * rows:(t + 1) * rows],
                                                win_b[:, r, :], start=True, stop=True)
                last.then_inc(products_ready[layer], 1)

            def sum_messages(layer, q, i, r):
                k, rows = shape_of(i, r)
                g = q * N_CHUNKS + RING * number(i) + r
                pe.wait_ge(sums_copied[layer], done(g))
                pe.wait_ge(onehot_ready[layer], g + 1)
                if layer:
                    pe.wait_ge(messages_ready, g + 1)
                else:
                    pe.wait_ge(mixed[0], done(g + 1))
                for t in range(k):
                    last = nc.tensor.matmul(ps_sum, gath[0:rows, r, t, :], onehot[0:rows, r % 2, t, :],
                                            start=(t == 0), stop=(t == k - 1))
                if layer == 1:
                    oh = onehot[0:rows, r % 2, 0:k, :].bitcast(BF16)
                    for t in range(k):
                        last = nc.tensor.matmul(ps_deg, ones_h[0:rows, :], oh[:, t, 1:2 * WINDOW:2],
                                                 start=(t == 0), stop=(t == k - 1))
                last.then_inc(summed[layer], 1)

            def project(layer, g):
                pe.wait_ge(sums_copied[layer], done(g + 1))
                pe.wait_ge(acc_added[layer], done(g))
                if layer == 0:
                    nc.tensor.matmul(ps_proj, w1_s[:, :], sums[:, :], start=True, stop=True).then_inc(projected[0], 1)
                    return
                nc.tensor.matmul(ps_proj, m2_s[:, :], sums[:, :], start=True, stop=False)
                nc.tensor.matmul(ps_proj, mb2_s[:, :], deg[:, :], start=False, stop=True).then_inc(projected[1], 1)
                pe.wait_ge(projection_copied, g + 1)
                nc.tensor.matmul(ps_proj2, m3b_s[:, :], sums2[:, :], start=True, stop=True).then_inc(updated, 1)

            def edge_sweeps(layer):
                def step(q, i, r, first=False):
                    if not first:
                        project(layer, q * N_CHUNKS + RING * number(i) + r - 1)
                    if layer and following(i, r):
                        turn(q, *following(i, r))
                    sum_messages(layer, q, i, r)
                    if following(i, r):
                        products(layer, q, *following(i, r))

                with pe.Fori(0, n_sweeps) as q:
                    if layer:
                        turn(q, 0, 0)
                    products(layer, q, 0, 0)
                    for r in range(RING):
                        step(q, 0, r, first=(r == 0))
                    with pe.Fori(1, GROUPS - 1) as i:
                        for r in range(RING):
                            step(q, i, r)
                    for r in range(RING):
                        step(q, LAST, r)
                    project(layer, (q + 1) * N_CHUNKS - 1)

            edge_sweeps(0)

            def piece_products(n, weights, ready, read, finished):
                for m in range(PIECE_BLOCKS):
                    j = n * PIECE_BLOCKS + m
                    if m == 0:
                        pe.wait_ge(read, done(j))
                    pe.wait_ge(ready, j + 1)
                    for t in range(BT):
                        last = nc.tensor.matmul(psum[0:ROWS, m, t * HID:(t + 1) * HID],
                                                u_buf[m][:, t * ROWS:(t + 1) * ROWS], weights, start=True, stop=True)
                    last.then_inc(finished, 1)

            with pe.Fori(0, PIECES) as n:
                piece_products(n, w2_s[:, :], u_ready, x2_ready, w2_done)

            def turn_h(j):
                pe.wait_ge(ht_copied, done(j))
                pe.wait_ge(h2_ready, j + 1)
                for t in range(BT):
                    last = nc.tensor.transpose(ps_t[:, t * ROWS:(t + 1) * ROWS], h_buf[:, t * HID:(t + 1) * HID],
                                               ident[0:ROWS, 0:ROWS])
                last.then_inc(ht_ready, 1)

            def times_w1_w3(j, m):
                pe.wait_ge(ht_copied, done(j + 1))
                pe.wait_ge(b_ready, done(j))
                for t in range(BT):
                    last = nc.tensor.matmul(ps_ab[:, t, :], ht_buf[m][:, t * ROWS:(t + 1) * ROWS],
                                            m1ab_s[:, :, :].rearrange("p a f -> p (a f)"), start=True, stop=True)
                last.then_inc(ab_done, 1)
                pe.wait_ge(c_ready, done(j))
                nc.tensor.matmul(ps_c, m3a_s[:, :], ht_buf[m], start=True, stop=True).then_inc(c_done, 1)

            turn_h(0)
            with pe.Fori(0, BLOCKS // 2) as i:
                for m in range(2):
                    turn_h(2 * i + m + 1)
                    times_w1_w3(2 * i + m, m)
            times_w1_w3(BLOCKS - 1, 0)

            edge_sweeps(1)

            with pe.Fori(0, PIECES) as n:
                piece_products(n, m4_s[:, :], v_ready, y_ready, w4_done)


def kernel(**inputs):
    import concourse.bacc as _bacc
    from concourse.bass_utils import run_bass_kernel_spmd as _run

    a = {k: np.asarray(v) for k, v in inputs.items()}
    full = FULL * CHUNK

    def by_chunk(v):
        return v[:full].reshape(FULL * P, K), v[full:].reshape(TAIL_ROWS, TAIL_K)

    def features(v):
        n = v.shape[1]
        body = v[:full].reshape(FULL, P, K, n).transpose(0, 3, 2, 1).reshape(FULL * n, CHUNK)
        tail = v[full:].reshape(TAIL_ROWS, TAIL_K, n).transpose(2, 1, 0).reshape(n, TAIL)
        return body, tail

    (src, src_tail), (dst, dst_tail) = by_chunk(a["src"]), by_chunk(a["dst"])
    rbf, rbf_tail = features(a["edge_attr_6"])
    ef, ef_tail = features(a["edge_attr_16"])
    laid = {
        "x": a["x"], "dst": a["dst"],
        "ids": np.concatenate([src, dst], axis=1), "ids_tail": np.concatenate([src_tail, dst_tail], axis=1),
        "rbf": rbf, "rbf_tail": rbf_tail, "ef": ef, "ef_tail": ef_tail,
        "w_rbf_t": a["L0_gnn_W_rbf"].T, "w1_t": a["L0_gnn_W1"].T, "b1": a["L0_gnn_b1"][:, None],
        "w2_t": a["L0_gnn_W2"].T, "b2": a["L0_gnn_b2"][None, :],
        "m1": a["L1_gnn_W1"], "mb1": a["L1_gnn_b1"][None, :], "m2": a["L1_gnn_W2"], "mb2": a["L1_gnn_b2"][None, :],
        "m3": a["L1_gnn_W3"], "mb3": a["L1_gnn_b3"][:, None], "m4": a["L1_gnn_W4"], "mb4": a["L1_gnn_b4"][None, :],
    }
    nc = _bacc.Bacc("TRN2", target_bir_lowering=False, num_devices=1)
    arrays, args = {}, []
    for name, v in laid.items():
        v = np.ascontiguousarray(v)
        arrays[f"in_{name}"] = v
        args.append(nc.dram_tensor(f"in_{name}", v.shape, mybir.dt.from_np(v.dtype), kind="ExternalInput").ap())
    out = nc.dram_tensor("out_0", (N_NODES, HID), F32, kind="ExternalOutput").ap()
    gnn_kernel(nc, *args, out)
    r = _run(nc, [arrays], core_ids=[0])
    return r.results[0]["out_0"]
```

```python
from contextlib import ExitStack

import numpy as np
import concourse.bass as bass
from concourse import mybir

F32 = mybir.dt.float32
BF16 = mybir.dt.bfloat16
I32 = mybir.dt.int32
ALU = mybir.AluOpType
ACT = mybir.ActivationFunctionType
AX_X = mybir.AxisListType.X

N_NODES, N_EDGES, HID = 12500, 200000, 128
N_RBF, N_EF = 6, 16
LN_EPS = 1e-5
RSQRT_SEED, NEWTON = 0x5F3759DF, 3
P = 128
ROWS = 125
NODE_TILES = N_NODES // ROWS
BT = 4
SPLIT = ROWS // 16 * 16
BN = BT * ROWS
BLOCKS = NODE_TILES // BT
PIECES = 5
PIECE_TILES = NODE_TILES // PIECES
PIECE_BLOCKS = BLOCKS // PIECES
POOL_TILES, DVE_TILES = BT, 2 * BT
K = 8
CHUNK = K * P
FULL = N_EDGES // CHUNK
TAIL = N_EDGES - FULL * CHUNK
TAIL_K = 4
TAIL_ROWS = TAIL // TAIL_K
N_CHUNKS = FULL + 1
RING = 4
GROUPS = N_CHUNKS // RING
OCTET = 2 * RING
OCTETS = GROUPS // 2
LEAD = 2
LAST_LEAD = 2
LEFT = BLOCKS - (OCTETS - 1)
WINDOW = P - N_EF
MIN_P = FULL // 3
assert OCTETS * 2 + 1 == GROUPS and LEFT == 2
assert TAIL_K * TAIL_ROWS == TAIL and GROUPS * RING == N_CHUNKS and MIN_P * 3 == FULL


def gnn_kernel(nc, x, dst, ids, ids_tail, rbf, rbf_tail, ef, ef_tail, w_rbf_t, w1_t, b1, w2_t, b2,
               m1, mb1, m2, mb2, m3, mb3, m4, mb4, out):
    h_table = nc.dram_tensor("h_table", (N_NODES, HID), F32).ap()
    a_table = nc.dram_tensor("a_table", (N_NODES, HID), F32).ap()
    b_table = nc.dram_tensor("b_table", (N_NODES + WINDOW, HID), F32).ap()
    lo_table = nc.dram_tensor("lo_table", (1, N_CHUNKS), F32).ap()
    hi_table = nc.dram_tensor("hi_table", (1, N_CHUNKS), F32).ap()

    with ExitStack() as ctx:
        def sb(name, shape, dt=F32):
            return ctx.enter_context(nc.sbuf_tensor(name, shape, dt))

        def sem(name):
            return ctx.enter_context(nc.semaphore(name))

        def sems(name, n):
            return [sem(f"{name}{i}") for i in range(n)]

        acc = sb("acc", [P, N_NODES + WINDOW])
        node_x = sb("node_x", [ROWS, NODE_TILES * HID])
        node_h = sb("node_h", [P, NODE_TILES * HID])
        gath = sb("gath", [P, RING, K, HID])
        lhs = sb("lhs", [P, RING, CHUNK])
        onehot = sb("onehot", [P, 2, K, WINDOW])
        win_b = sb("win_b", [P, RING, HID])
        idst = sb("idst", [P, RING, 2 * K], I32)
        rel = sb("rel", [P, 2, K])
        iota_w = sb("iota_w", [P, WINDOW])
        chunk_lo = sb("chunk_lo", [P, N_CHUNKS])
        win_lo = sb("win_lo", [P, N_CHUNKS])
        base_i = sb("base_i", [1, N_CHUNKS], I32)
        hi_row = sb("hi_row", [1, N_CHUNKS])
        lo3 = sb("lo3", [MIN_P, 3])
        hi3 = sb("hi3", [MIN_P, 3])
        lo_t = sb("lo_t", [1, 1])
        hi_t = sb("hi_t", [1, 1])
        span = sb("span", [1, N_CHUNKS])
        span_max = sb("span_max", [1, 1])
        span_i = sb("span_i", [1, 1], I32)
        start_node = sb("start_node", [1, OCTET * (OCTETS + 1)])
        slack = sb("slack", [1, N_CHUNKS])
        slack_min = sb("slack_min", [1, 1])
        span_slack = sb("span_slack", [1, 1])
        early_i = sb("early_i", [1, 1], I32)
        warm = sb("warm", [1, 1])
        sums = sb("sums", [P, WINDOW])
        sums2 = sb("sums2", [P, WINDOW])
        deg = sb("deg", [1, WINDOW])
        ident = sb("ident", [P, P])
        ident_h = sb("ident_h", [P, P], BF16)
        ones_h = sb("ones_h", [P, 1], BF16)
        stats = sb("stats", [ROWS, PIECE_TILES, 6])
        half_sum = sb("half_sum", [ROWS, PIECE_TILES])
        diff = sb("diff", [ROWS, PIECE_TILES])
        squares = sb("squares", [ROWS, PIECE_TILES])
        neg_mean = sb("neg_mean", [ROWS, PIECE_TILES])
        var_eps = sb("var_eps", [ROWS, PIECE_TILES])
        newton = sb("newton", [ROWS, PIECE_TILES])
        seed = sb("seed", [ROWS, PIECE_TILES], I32)
        rstd = sb("rstd", [ROWS, NODE_TILES])
        nmr = sb("nmr", [ROWS, NODE_TILES])
        w_rbf_s = sb("w_rbf_s", [N_RBF, HID])
        w1_s = sb("w1_s", [P, HID])
        w2_s = sb("w2_s", [P, HID])
        m1a_s = sb("m1a_s", [P, HID])
        m1b_s = sb("m1b_s", [P, HID])
        m2_s = sb("m2_s", [P, HID])
        m3a_s = sb("m3a_s", [P, HID])
        m3b_s = sb("m3b_s", [P, HID])
        m4_s = sb("m4_s", [P, HID])
        b1_s = sb("b1_s", [P, 1])
        mb3_s = sb("mb3_s", [P, 1])
        b2_s = sb("b2_s", [ROWS, HID])
        mb1_s = sb("mb1_s", [ROWS, HID])
        mb4_s = sb("mb4_s", [ROWS, HID])
        mb2_s = sb("mb2_s", [1, HID])
        psum = ctx.enter_context(nc.psum_tensor("psum", [P, 8, 512], F32))

        gflat = gath[:, :, :, :].rearrange("p r k f -> p (r k f)")
        dst3 = gflat[0:MIN_P, 0:3 * CHUNK].bitcast(I32).rearrange("p (k e) -> p k e", k=3)
        dst_t = gflat[0:1, 3 * CHUNK:3 * CHUNK + TAIL].bitcast(I32)
        lflat = lhs[:, :, :].rearrange("p r e -> p (r e)")
        u_buf = node_h[:, 0:BN]
        ht_buf = node_h[:, 512:512 + BN]
        h_buf = node_h[0:ROWS, 1024:1536]
        a_stage = node_h[0:ROWS, 1536:2048]
        b_stage = node_h[0:ROWS, 2048:2560]
        zeros = onehot[:, :, :, :].rearrange("p a k w -> p (a k w)")[0:WINDOW, 0:HID]
        ps_pre = psum[:, 0:2, :].rearrange("p a (k f) -> p (a k) f", f=HID)
        ps_oht = psum[:, 2, :].bitcast(BF16)
        ps_sum = psum[:, 3, 0:WINDOW]
        ps_deg = psum[0:1, 3, 256:256 + WINDOW]
        ps_proj = psum[:, 4, 0:WINDOW]
        ps_proj2 = psum[:, 5, 0:WINDOW]
        ps_w2 = psum[0:ROWS, 5, :]
        ps_t = psum[:, 5, 0:BN]
        ps_c = psum[:, 2, 0:BN]
        ps_a, ps_b = psum[0:ROWS, 6, :], psum[0:ROWS, 7, :]
        ps_w4 = psum[0:ROWS, 6, :]

        def node_tiles(ap, j0, n):
            return ap[0:ROWS, bass.ds(j0 * HID, n * HID)]

        def table_rows(t, j0, n):
            return t[bass.ds(j0 * ROWS, n * ROWS), :].rearrange("(j p) f -> p j f", p=ROWS)

        def store_nodes(eng, table, j0, n, tile, done):
            dram = table_rows(table, j0, n)
            on_chip = tile.rearrange("p (j f) -> p j f", f=HID)
            for lo, hi in ((0, SPLIT), (SPLIT, ROWS)):
                eng.dma_start(dram[lo:hi], on_chip[lo:hi]).then_inc(done, 16)

        waited = {name: sem(f"waited_{name}") for name in ("dve", "pool", "sp", "act")}
        x_loaded = sems("x_loaded", PIECES)
        dst_loaded = sem("dst_loaded")
        weights_loaded = sem("weights_loaded")
        extremes_ready = sem("extremes_ready")
        extremes_stored = sem("extremes_stored")
        extremes_loaded = sem("extremes_loaded")
        span_steps = sem("span_steps")
        span_ready = sem("span_ready")
        consts_ready = sem("consts_ready")
        ident_zero = sem("ident_zero")
        ident_ready = sem("ident_ready")
        acc_zeroed = sem("acc_zeroed")
        zeros_ready = sem("zeros_ready")
        zeros_stored = sem("zeros_stored")
        stats_step = sem("stats_step")
        norm_ready = sem("norm_ready")
        h_ready = sem("h_ready")
        pool_h_step = sem("pool_h_step")
        pool_h_ready = sem("pool_h_ready")
        dve_h_step = sem("dve_h_step")
        dve_h_ready = sem("dve_h_ready")
        h_stored = sem("h_stored")
        bias_added = sem("bias_added")
        summed = sems("summed", 2)
        ids_loaded = [sems(f"ids_loaded{l}_", RING) for l in range(2)]
        feats_loaded = [sems(f"feats_loaded{l}_", RING) for l in range(2)]
        gathered = [sems(f"gathered{l}_", RING) for l in range(2)]
        counted_anew = sems("counted_anew", 2)
        window_step = sems("window_step", 2)
        window_ready = sems("window_ready", 2)
        rel_ready = sems("rel_ready", 2)
        onehot_ready = sems("onehot_ready", 2)
        turned = sem("turned")
        turned_copied = sem("turned_copied")
        products_ready = sems("products_ready", 2)
        mixed = sems("mixed", 2)
        messages_ready = sem("messages_ready")
        sums_copied = sems("sums_copied", 2)
        projected = sems("projected", 2)
        projection_copied = sem("projection_copied")
        updated = sem("updated")
        acc_added = sems("acc_added", 2)
        u_ready = sem("u_ready")
        w2_done = sem("w2_done")
        x2_ready = sem("x2_ready")
        stats2_step = sem("stats2_step")
        norm2_ready = sem("norm2_ready")
        h2_ready = sem("h2_ready")
        xh_step = sem("xh_step")
        xh_ready = sem("xh_ready")
        ht_ready = sem("ht_ready")
        ht_copied = sem("ht_copied")
        a_done = sem("a_done")
        b_done = sem("b_done")
        c_done = sem("c_done")
        a_ready = sem("a_ready")
        b_ready = sem("b_ready")
        c_ready = sem("c_ready")
        a_stored = sem("a_stored")
        b_stored = sem("b_stored")
        v_ready = sem("v_ready")
        w4_done = sem("w4_done")
        y_ready = sem("y_ready")
        out_stored = sem("out_stored")

        N_WEIGHTS = 15 + RING
        H_STORES = 32 * (PIECES + 2)
        ACT_J0 = NODE_TILES - PIECE_TILES
        POOL_J0 = NODE_TILES - POOL_TILES
        DVE_J0 = POOL_J0 - DVE_TILES

        def act_blocks_done(n):
            return min(PIECE_BLOCKS * (n + 1), DVE_J0 // BT)

        from_one = [*mixed, *acc_added, *sums_copied, turned_copied, w2_done, x2_ready, ht_copied,
                    xh_ready, b_ready, c_ready, a_stored, b_stored, w4_done, y_ready]

        def done(n):
            return n + 1

        def sweeps(eng):
            eng.wait_ge(span_ready, 2)
            widest = eng.value_load(span_i[0:1, 0:1], min_val=0, max_val=N_NODES - 1)
            return widest // WINDOW + 1

        def steer(eng):
            return eng.value_load(early_i[0:1, 0:1], min_val=0, max_val=1)

        def shape_of(i, r):
            return (TAIL_K, TAIL_ROWS) if i is LAST and r == RING - 1 else (K, P)

        LAST = "last"

        def number(i):
            return GROUPS - 1 if i is LAST else i

        def following(i, r):
            if r + 1 < RING:
                return i, r + 1
            return None if i is LAST else (i + 1, 0)

        def gathered_count(i, r):
            return 16 * K * number(i) + 16 * shape_of(i, r)[0]

        block = ctx.enter_context(nc.Block())

        @block.sync
        def _(sp):
            def load_nodes(tile, table, j0, n, done):
                dram = table_rows(table, j0, n)
                on_chip = tile.rearrange("p (j f) -> p j f", f=HID)
                for lo, hi in ((0, SPLIT), (SPLIT, ROWS)):
                    sp.dma_start(on_chip[lo:hi], dram[lo:hi]).then_inc(done, 16)

            for n in range(PIECES):
                if n == 1:
                    sp.dma_start(dst3, dst[0:FULL * CHUNK].rearrange("(p k e) -> p k e", k=3, e=CHUNK)
                                 ).then_inc(dst_loaded, 16)
                    sp.dma_start(dst_t, dst[FULL * CHUNK:N_EDGES].rearrange("(a e) -> a e", a=1)
                                 ).then_inc(dst_loaded, 16)
                load_nodes(node_tiles(node_x, n * PIECE_TILES, PIECE_TILES), x, n * PIECE_TILES, PIECE_TILES,
                           x_loaded[n])
            for tile, src in ((w_rbf_s[:, :], w_rbf_t), (w1_s[:, :], w1_t), (w2_s[:, :], w2_t),
                              (m1a_s[:, :], m1[0:HID, :]), (m1b_s[:, :], m1[HID:2 * HID, :]),
                              (m2_s[:, :], m2), (m3a_s[:, :], m3[0:HID, :]), (m3b_s[:, :], m3[HID:2 * HID, :]),
                              (m4_s[:, :], m4), (b1_s[:, :], b1), (mb3_s[:, :], mb3), (mb2_s[:, :], mb2),
                              (b2_s[:, :], b2.partition_broadcast(ROWS)), (mb1_s[:, :], mb1.partition_broadcast(ROWS)),
                              (mb4_s[:, :], mb4.partition_broadcast(ROWS))):
                sp.dma_start(tile, src).then_inc(weights_loaded, 16)
            for r in range(RING):
                sp.dma_start(win_b[WINDOW:P, r, :], m1[2 * HID:2 * HID + N_EF, :]).then_inc(weights_loaded, 16)
            sp.wait_ge(extremes_ready, 4)
            sp.dma_start(lo_table[0, 0:FULL].rearrange("(p k) -> p k", k=3), lo3[:, :]).then_inc(extremes_stored, 16)
            sp.dma_start(hi_table[0, 0:FULL].rearrange("(p k) -> p k", k=3), hi3[:, :]).then_inc(extremes_stored, 16)
            sp.dma_start(lo_table[:, FULL:N_CHUNKS], lo_t[:, :]).then_inc(extremes_stored, 16)
            sp.dma_start(hi_table[:, FULL:N_CHUNKS], hi_t[:, :]).then_inc(extremes_stored, 16)
            sp.wait_ge(extremes_stored, 64)
            sp.dma_start(chunk_lo[:, :], lo_table.partition_broadcast(P)).then_inc(extremes_loaded, 16)
            sp.dma_start(hi_row[:, :], hi_table).then_inc(extremes_loaded, 16)
            sp.wait_ge(zeros_ready, 1)
            sp.dma_start(b_table[N_NODES:N_NODES + WINDOW, :], zeros).then_inc(zeros_stored, 16)
            for n in range(PIECES - 1):
                sp.wait_ge(h_ready, act_blocks_done(n))
                store_nodes(sp, h_table, n * PIECE_TILES, PIECE_TILES, node_tiles(node_h, n * PIECE_TILES, PIECE_TILES),
                            h_stored)
            for ready, count, j0, n in ((dve_h_ready, 1, DVE_J0, DVE_TILES),
                                        (h_ready, act_blocks_done(PIECES - 1), ACT_J0, DVE_J0 - ACT_J0),
                                        (pool_h_ready, 1, POOL_J0, POOL_TILES)):
                sp.wait_ge(ready, count)
                store_nodes(sp, h_table, j0, n, node_tiles(node_h, j0, n), h_stored)

            n_sweeps = sweeps(sp)
            early = steer(sp)

            def load_chunk(layer, q, i, r):
                k, rows = shape_of(i, r)
                c = RING * number(i) + r
                sp.wait_ge(summed[layer], q * N_CHUNKS + c + 1)
                tail = k != K
                ids_src = ids_tail if tail else ids[bass.ds(c * P, P), :]
                sp.dma_start(idst[0:rows, r, 0:2 * k], ids_src).then_inc(ids_loaded[layer][r], 16)
                if layer == 0:
                    src = rbf_tail if tail else rbf[bass.ds(c * N_RBF, N_RBF), :]
                    sp.dma_start(lhs[0:N_RBF, r, 0:k * rows], src).then_inc(feats_loaded[0][r], 16)
                else:
                    src = ef_tail if tail else ef[bass.ds(c * N_EF, N_EF), :]
                    sp.dma_start(lhs[WINDOW:P, r, 0:k * rows], src).then_inc(feats_loaded[1][r], 16)
                    sp.wait_ge(b_stored, done(32 * BLOCKS))
                    base = sp.value_load(base_i[0:1, bass.ds(c, 1)], min_val=0, max_val=N_NODES)
                    sp.dma_start(win_b[0:WINDOW, r, :], b_table[bass.ds(base, WINDOW), :]
                                 ).then_inc(feats_loaded[1][r], 16)

            def store_a(j):
                sp.wait_ge(a_ready, j + 1)
                store_nodes(sp, a_table, j * BT, BT, a_stage, a_stored)

            def store_out(j):
                sp.wait_ge(y_ready, done(j + 1))
                store_nodes(sp, out, j * BT, BT, node_tiles(node_x, j * BT, BT), out_stored)

            def edge_sweeps(layer, store_block):
                with sp.Fori(0, n_sweeps) as q:
                    sp.wait_ge(window_ready[layer], q + 1)
                    sp.sem_inc(waited["sp"], 1)
                    for s in range(2 * OCTET):
                        load_chunk(layer, q, s // RING, s % RING)
                    with sp.Fori(2, OCTETS) as p:
                        for s in range(OCTET):
                            load_chunk(layer, q, 2 * p + s // RING, s % RING)
                            if s == RING:
                                with sp.If(early > 0):
                                    store_block(p - 2)
                    for r in range(RING):
                        load_chunk(layer, q, LAST, r)
                with sp.Fori(early * (BLOCKS - LEFT - 1), BLOCKS) as j:
                    store_block(j)

            edge_sweeps(0, store_a)
            sp.wait_ge(zeros_stored, 16)
            edge_sweeps(1, store_out)
            sp.wait_ge(out_stored, 32 * BLOCKS)
            sp.wait_ge(h_stored, H_STORES)
            sp.wait_ge(weights_loaded, 16 * N_WEIGHTS)

        @block.gpsimd
        def _(pool):
            nc.gpsimd.iota(iota_w[:, :], pattern=[[1, WINDOW]], base=0, channel_multiplier=0,
                           allow_small_or_imprecise_dtypes=True).then_inc(consts_ready, 1)
            nc.gpsimd.iota(start_node[:, :].rearrange("p (a b) -> p a b", b=OCTET),
                           pattern=[[BN, OCTETS + 1], [0, OCTET]], base=0, channel_multiplier=0,
                           allow_small_or_imprecise_dtypes=True).then_inc(consts_ready, 1)
            nc.gpsimd.memset(ones_h[:, :], 1.0).then_inc(consts_ready, 1)
            nc.gpsimd.memset(ident[:, :], 0.0).then_inc(ident_zero, 1)
            nc.gpsimd.memset(ident_h[:, :], 0.0).then_inc(ident_zero, 1)
            nc.gpsimd.memset(zeros, 0.0).then_inc(zeros_ready, 1)
            pool.wait_ge(ident_zero, 2)
            nc.gpsimd.affine_select(out=ident[:, :], in_=ident[:, :], compare_op=ALU.not_equal, fill=1.0,
                                    base=0, pattern=[[-1, P]], channel_multiplier=1).then_inc(ident_ready, 1)
            nc.gpsimd.affine_select(out=ident_h[:, :], in_=ident_h[:, :], compare_op=ALU.not_equal, fill=1.0,
                                    base=0, pattern=[[-1, P]], channel_multiplier=1).then_inc(ident_ready, 1)

            nc.gpsimd.memset(acc[:, :], 0.0).then_inc(acc_zeroed, 1)

            pool.wait_ge(norm_ready, PIECES)
            for j in range(POOL_J0, NODE_TILES):
                nc.gpsimd.tensor_scalar(node_h[0:ROWS, j * HID:(j + 1) * HID], node_x[:, j * HID:(j + 1) * HID],
                                        rstd[:, j:j + 1], nmr[:, j:j + 1], ALU.mult, ALU.add
                                        ).then_inc(pool_h_step, 1)
            pool.wait_ge(pool_h_step, POOL_TILES)
            hv = node_tiles(node_h, POOL_J0, POOL_TILES)
            nc.gpsimd.tensor_scalar(hv, hv, 0.0, None, ALU.max).then_inc(pool_h_ready, 1)

            n_sweeps = sweeps(pool)

            def gather_group(layer, table, q, i):
                for r in range(RING):
                    k, rows = shape_of(i, r)
                    pool.wait_ge(ids_loaded[layer][r], 16 * (q * GROUPS + number(i) + 1))
                    pool.sem_inc(waited["pool"], 1)
                    for t in range(k):
                        pool.indirect_dma_start(
                            out=gath[0:rows, r, t, :], out_offset=None, in_=table,
                            in_offset=bass.IndirectOffsetOnAxis(ap=idst[0:rows, r, t:t + 1], axis=0),
                        ).then_inc(gathered[layer][r], 16)

            def edge_sweeps(layer, table):
                pool.sem_inc(counted_anew[layer], 1)
                with pool.Fori(0, n_sweeps) as q:
                    with pool.Fori(0, GROUPS - 1) as i:
                        gather_group(layer, table, q, i)
                    gather_group(layer, table, q, LAST)
                    for r in range(RING):
                        pool.wait_ge(gathered[layer][r], gathered_count(LAST, r))
                    pool.wait_ge(mixed[layer], done((q + 1) * N_CHUNKS))
                    pool.sem_inc(waited["pool"], 1)
                    nc.gpsimd.inc_swdge_sem(gathered[layer], [gathered_count(LAST, r) for r in range(RING)],
                                            mode="sub")
                    pool.sem_inc(counted_anew[layer], 1)

            pool.wait_ge(h_stored, H_STORES)
            edge_sweeps(0, h_table)
            pool.wait_ge(a_stored, done(32 * BLOCKS))
            edge_sweeps(1, a_table)

        @block.scalar
        def _(act):
            for s in from_one:
                act.sem_inc(s, 1)

            def normalise(j):
                for t in range(BT):
                    col = bass.ds(j * BT + t, 1)
                    last = nc.scalar.activation(node_tiles(node_h, j * BT + t, 1), node_tiles(node_x, j * BT + t, 1),
                                                ACT.Relu, bias=nmr[:, col], scale=rstd[:, col])
                last.then_inc(h_ready, 1)

            for n in range(PIECES):
                act.wait_ge(norm_ready, n + 1)
                normalise(n * PIECE_BLOCKS)
                with act.Fori(n * PIECE_BLOCKS + 1, act_blocks_done(n)) as j:
                    normalise(j)

            n_sweeps = sweeps(act)
            early = steer(act)

            def copy_sums(layer, g):
                act.wait_ge(summed[layer], RING + g + 1)
                if layer == 1:
                    nc.scalar.copy(deg[:, :], ps_deg)
                nc.scalar.copy(sums[:, :], ps_sum).then_inc(sums_copied[layer], 1)

            def silu_block(j, layer, bias):
                act.wait_ge(w4_done if layer else w2_done, done(j))
                act.sem_inc(waited["act"], 1)
                nc.scalar.activation(u_buf, acc[:, bass.ds(j * BN, BN)], ACT.Silu, **bias
                                     ).then_inc(v_ready if layer else u_ready, 1)

            def normalise2(j):
                act.wait_ge(norm2_ready, j + 1)
                act.wait_ge(xh_ready, done(j))
                act.sem_inc(waited["act"], 1)
                for t in range(BT):
                    last = nc.scalar.activation(h_buf[:, t * HID:(t + 1) * HID], node_tiles(node_x, j * BT + t, 1),
                                                ACT.Relu, bias=nmr[:, t:t + 1], scale=rstd[:, t:t + 1])
                last.then_inc(h2_ready, 1)

            def copy_ht(j):
                act.wait_ge(ht_ready, j + 1)
                nc.scalar.copy(ht_buf, ps_t).then_inc(ht_copied, 1)

            def keep_c(j):
                act.wait_ge(c_done, j + 1)
                act.sem_inc(waited["act"], 1)
                nc.scalar.activation(acc[:, bass.ds(j * BN, BN)], ps_c, ACT.Identity, bias=mb3_s[:, 0:1]
                                     ).then_inc(c_ready, 1)

            def store_b(j):
                act.wait_ge(b_ready, done(j + 1))
                store_nodes(act, b_table, j * BT, BT, b_stage, b_stored)

            def block_part0(s, j, q=None):
                if s == 2:
                    if q is not None:
                        act.wait_ge(acc_added[0], done(q * N_CHUNKS + OCTET * (j + 1) + LEAD))
                    silu_block(j, 0, {"bias": b1_s[:, 0:1]})
                if s == 5:
                    normalise2(j)
                    copy_ht(j)
                if s == 7:
                    keep_c(j)
                if s == 8:
                    store_b(j)

            with act.Fori(0, n_sweeps) as q:
                for s in range(OCTET):
                    copy_sums(0, q * N_CHUNKS + s)
                with act.Fori(1, OCTETS) as p:
                    for s in range(OCTET):
                        copy_sums(0, q * N_CHUNKS + p * OCTET + s)
                        if s in (2, 5, 7):
                            with act.If(early > 0):
                                block_part0(s, p - 1, q)
                                if s == 7:
                                    block_part0(8, p - 1)
                with act.If(early > 0):
                    act.wait_ge(acc_added[0], done(q * N_CHUNKS + OCTETS * OCTET - LAST_LEAD))
                    block_part0(2, BLOCKS - LEFT)
                for r in range(RING):
                    copy_sums(0, q * N_CHUNKS + OCTETS * OCTET + r)
                    for last_r, s in ((0, 5), (2, 8), (2, 7)):
                        if r == last_r:
                            with act.If(early > 0):
                                block_part0(s, BLOCKS - LEFT)
            nc.scalar.activation(warm[:, :], b1_s[0:1, 0:1], ACT.Silu)
            act.wait_ge(acc_added[0], done(n_sweeps * N_CHUNKS))
            with act.Fori(early * (BLOCKS - 1), BLOCKS) as j:
                for s in (2, 5, 7, 8):
                    block_part0(s, j)

            def copy_turned(q, i, r):
                k, rows = shape_of(i, r)
                g = q * N_CHUNKS + RING * number(i) + r
                act.wait_ge(feats_loaded[1][r], 32 * (q * GROUPS + number(i) + 1))
                act.wait_ge(turned, g + 1)
                nc.scalar.copy(lhs[0:WINDOW, r, 0:k * rows], ps_oht[0:WINDOW, 0:k * rows]).then_inc(turned_copied, 1)

            def silu_messages(q, i, r):
                k, rows = shape_of(i, r)
                act.wait_ge(mixed[1], done(q * N_CHUNKS + RING * number(i) + r + 1))
                nc.scalar.activation(gath[0:rows, r, 0:k, :], gath[0:rows, r, 0:k, :], ACT.Silu
                                     ).then_inc(messages_ready, 1)

            def copy_projection(g):
                act.wait_ge(projected[1], g + 1)
                nc.scalar.copy(sums2[:, :], ps_proj).then_inc(projection_copied, 1)

            def step(q, i, r, first=False):
                g = q * N_CHUNKS + RING * number(i) + r
                if not first:
                    copy_projection(g - 1)
                silu_messages(q, i, r)
                if following(i, r):
                    copy_turned(q, *following(i, r))
                copy_sums(1, g)

            with act.Fori(0, n_sweeps) as q:
                copy_turned(q, 0, 0)
                for s in range(OCTET):
                    step(q, s // RING, s % RING, first=(s == 0))
                with act.Fori(1, OCTETS) as p:
                    for s in range(OCTET):
                        step(q, 2 * p + s // RING, s % RING)
                        if s == 2:
                            with act.If(early > 0):
                                act.wait_ge(acc_added[1], done(q * N_CHUNKS + OCTET * p + LEAD))
                                silu_block(p - 1, 1, {})
                with act.If(early > 0):
                    act.wait_ge(acc_added[1], done(q * N_CHUNKS + OCTETS * OCTET - LAST_LEAD))
                    silu_block(BLOCKS - LEFT, 1, {})
                for r in range(RING):
                    step(q, LAST, r)
                copy_projection((q + 1) * N_CHUNKS - 1)
            act.wait_ge(acc_added[1], done(n_sweeps * N_CHUNKS))
            with act.Fori(early * (BLOCKS - 1), BLOCKS) as j:
                silu_block(j, 1, {})

        @block.vector
        def _(dve):
            def tile_stats(j0, n):
                for t in range(n):
                    last = nc.vector.bn_stats(stats[:, t, :], node_tiles(node_x, j0 + t, 1))
                return last

            def rstd_of(n, at, step, before, ready):
                count = [before]

                def after(*instructions):
                    for ins in instructions:
                        ins.then_inc(step, 1)
                    count[0] += len(instructions)
                    dve.wait_ge(step, count[0])

                dve.wait_ge(step, before)
                mean_e, sq_e = stats[:, 0:n, 1], stats[:, 0:n, 2]
                mean_o, sq_o = stats[:, 0:n, 4], stats[:, 0:n, 5]
                hs, df, sq, nm = half_sum[:, 0:n], diff[:, 0:n], squares[:, 0:n], neg_mean[:, 0:n]
                ve, y, t = var_eps[:, 0:n], rstd[:, at:at + n], newton[:, 0:n]
                after(nc.vector.tensor_scalar(hs, mean_o, -0.5, None, ALU.mult),
                      nc.vector.tensor_tensor(df, mean_e, mean_o, ALU.subtract),
                      nc.vector.tensor_tensor(sq, sq_e, sq_o, ALU.add))
                after(nc.vector.scalar_tensor_tensor(out=nm, in0=mean_e, scalar=-0.5, in1=hs,
                                                     op0=ALU.mult, op1=ALU.add),
                      nc.vector.scalar_tensor_tensor(out=ve, in0=df, scalar=0.25, in1=df,
                                                     op0=ALU.mult, op1=ALU.mult),
                      nc.vector.tensor_scalar(sq, sq, 1.0 / HID, LN_EPS, ALU.mult, ALU.add))
                after(nc.vector.tensor_tensor(ve, ve, sq, ALU.add))
                after(nc.vector.tensor_scalar(seed[:, 0:n], ve.bitcast(I32), 1, None, ALU.logical_shift_right))
                after(nc.vector.tensor_scalar(y.bitcast(I32), seed[:, 0:n], -1, RSQRT_SEED, ALU.mult, ALU.add))
                for _ in range(NEWTON):
                    after(nc.vector.tensor_tensor(t, y, y, ALU.mult))
                    after(nc.vector.scalar_tensor_tensor(out=t, in0=t, scalar=-0.5, in1=ve,
                                                         op0=ALU.mult, op1=ALU.mult))
                    after(nc.vector.scalar_tensor_tensor(out=y, in0=t, scalar=1.5, in1=y,
                                                         op0=ALU.add, op1=ALU.mult))
                nc.vector.tensor_tensor(nmr[:, at:at + n], nm, y, ALU.mult).then_inc(ready, 1)

            RSTD_STEPS = 9 + 3 * NEWTON
            for n in range(PIECES):
                if n == 1:
                    dve.wait_ge(dst_loaded, 32)
                    nc.vector.tensor_reduce(lo3[:, :], dst3, AX_X, ALU.min).then_inc(extremes_ready, 1)
                    nc.vector.tensor_reduce(hi3[:, :], dst3, AX_X, ALU.max).then_inc(extremes_ready, 1)
                    nc.vector.tensor_reduce(lo_t[:, :], dst_t, AX_X, ALU.min).then_inc(extremes_ready, 1)
                    nc.vector.tensor_reduce(hi_t[:, :], dst_t, AX_X, ALU.max).then_inc(extremes_ready, 1)
                dve.wait_ge(x_loaded[n], 32)
                tile_stats(n * PIECE_TILES, PIECE_TILES).then_inc(stats_step, 1)
                rstd_of(PIECE_TILES, n * PIECE_TILES, stats_step, n * (RSTD_STEPS + 1) + 1, norm_ready)
            dve.wait_ge(norm_ready, PIECES)
            for j in range(DVE_J0, POOL_J0):
                nc.vector.tensor_scalar(node_h[0:ROWS, j * HID:(j + 1) * HID], node_x[:, j * HID:(j + 1) * HID],
                                        rstd[:, j:j + 1], nmr[:, j:j + 1], ALU.mult, ALU.add).then_inc(dve_h_step, 1)
            dve.wait_ge(dve_h_step, DVE_TILES)
            hv = node_tiles(node_h, DVE_J0, DVE_TILES)
            nc.vector.tensor_scalar(hv, hv, 0.0, None, ALU.max).then_inc(dve_h_ready, 1)

            dve.wait_ge(extremes_loaded, 32)
            nc.vector.tensor_tensor(span[:, :], hi_row[:, :], chunk_lo[0:1, :], ALU.subtract).then_inc(span_steps, 1)
            dve.wait_ge(span_steps, 1)
            nc.vector.tensor_reduce(span_max[:, :], span[:, :], AX_X, ALU.max).then_inc(span_steps, 1)
            dve.wait_ge(span_steps, 2)
            nc.vector.tensor_copy(span_i[:, :], span_max[:, :]).then_inc(span_ready, 1)
            dve.wait_ge(consts_ready, 3)
            last = OCTET * OCTETS - LAST_LEAD
            nc.vector.tensor_tensor(slack[:, LEAD:last], chunk_lo[0:1, LEAD:last],
                                    start_node[:, 0:last - LEAD], ALU.subtract).then_inc(span_steps, 1)
            nc.vector.tensor_scalar(slack[:, last:N_CHUNKS], chunk_lo[0:1, last:N_CHUNKS],
                                    -float(BN * (BLOCKS - 1)), None, ALU.add).then_inc(span_steps, 1)
            nc.vector.tensor_scalar(span_slack[:, :], span_max[:, :], -1.0, float(WINDOW - 1), ALU.mult, ALU.add
                                    ).then_inc(span_steps, 1)
            dve.wait_ge(span_steps, 5)
            nc.vector.tensor_reduce(slack_min[:, :], slack[:, LEAD:N_CHUNKS], AX_X, ALU.min).then_inc(span_steps, 1)
            dve.wait_ge(span_steps, 6)
            nc.vector.tensor_tensor(slack_min[:, :], slack_min[:, :], span_slack[:, :], ALU.min
                                    ).then_inc(span_steps, 1)
            dve.wait_ge(span_steps, 7)
            nc.vector.tensor_scalar(early_i[:, :], slack_min[:, :], 0.0, None, ALU.is_ge).then_inc(span_ready, 1)

            n_sweeps = sweeps(dve)
            early = steer(dve)

            def base_row(layer):
                nc.vector.tensor_scalar(base_i[:, :], win_lo[0:1, :], float(N_NODES), None, ALU.min
                                        ).then_inc(window_ready[layer], 1)

            def build_onehot(layer, q, i, r, chunks_summed):
                k, rows = shape_of(i, r)
                c = RING * number(i) + r
                dve.wait_ge(ids_loaded[layer][r], 16 * (q * GROUPS + number(i) + 1))
                nc.vector.tensor_scalar(rel[0:rows, r % 2, 0:k], idst[0:rows, r, k:2 * k],
                                        win_lo[0:rows, bass.ds(c, 1)], None, ALU.subtract).then_inc(rel_ready[layer], 1)
                dve.wait_ge(summed[layer], RING + chunks_summed)
                dve.wait_ge(rel_ready[layer], q * N_CHUNKS + c + 1)
                nc.vector.tensor_tensor(onehot[0:rows, r % 2, 0:k, :],
                                        rel[0:rows, r % 2, 0:k].unsqueeze(2).broadcast_to([rows, k, WINDOW]),
                                        iota_w[0:rows, :].unsqueeze(1).broadcast_to([rows, k, WINDOW]),
                                        ALU.is_equal).then_inc(onehot_ready[layer], 1)

            def mix(layer, q, i, r):
                k, rows = shape_of(i, r)
                g = q * N_CHUNKS + RING * number(i) + r
                dve.wait_ge(products_ready[layer], g + 1)
                dve.wait_ge(gathered[layer][r], gathered_count(i, r))
                gv = gath[0:rows, r, 0:k, :]
                nc.vector.tensor_tensor(gv, gv, ps_pre[0:rows, 0:k, :], ALU.add if layer else ALU.mult
                                        ).then_inc(mixed[layer], 1)

            def add_window(layer, q, c):
                g = q * N_CHUNKS + c
                base = dve.value_load(base_i[0:1, bass.ds(c, 1)], min_val=0, max_val=N_NODES)
                dve.wait_ge(updated if layer else projected[0], g + 1)
                dve.wait_ge(acc_added[layer], done(g))
                av = acc[:, bass.ds(base, WINDOW)]
                nc.vector.tensor_tensor(av, av, ps_proj2 if layer else ps_proj, ALU.add
                                        ).then_inc(acc_added[layer], 1)

            def take_x2(j):
                dve.wait_ge(w2_done, done(j + 1))
                xb = node_tiles(node_x, j * BT, BT)
                nc.vector.tensor_tensor(xb, xb, ps_w2, ALU.add).then_inc(x2_ready, 1)
                dve.wait_ge(x2_ready, done(j + 1))
                dve.sem_inc(waited["dve"], 1)
                tile_stats(j * BT, BT).then_inc(stats2_step, 1)
                rstd_of(BT, 0, stats2_step, j * (RSTD_STEPS + 1) + 1, norm2_ready)

            def take_residual(j):
                dve.wait_ge(h2_ready, j + 1)
                xb = node_tiles(node_x, j * BT, BT)
                nc.vector.tensor_tensor(xb, xb, h_buf, ALU.add).then_inc(xh_step, 1)
                dve.wait_ge(xh_step, j + 1)
                xv = xb.rearrange("p (j f) -> p j f", f=HID)
                nc.vector.tensor_tensor(xv, xv, mb4_s[:, :].unsqueeze(1).broadcast_to([ROWS, BT, HID]), ALU.add
                                        ).then_inc(xh_ready, 1)

            def keep_ab(j):
                dve.wait_ge(a_done, j + 1)
                dve.wait_ge(a_stored, done(32 * j))
                nc.vector.tensor_copy(a_stage, ps_a).then_inc(a_ready, 1)
                dve.wait_ge(b_done, j + 1)
                dve.wait_ge(b_stored, done(32 * j))
                nc.vector.tensor_tensor(b_stage.rearrange("p (j f) -> p j f", f=HID),
                                        ps_b.rearrange("p (j f) -> p j f", f=HID),
                                        mb1_s[:, :].unsqueeze(1).broadcast_to([ROWS, BT, HID]), ALU.add
                                        ).then_inc(b_ready, 1)

            def block_part0(s, j):
                if s == 4:
                    take_x2(j)
                if s == 6:
                    take_residual(j)
                if s == 7:
                    keep_ab(j)

            def block_part1(s, j):
                if s == 4:
                    dve.wait_ge(w4_done, done(j + 1))
                    xb = node_tiles(node_x, j * BT, BT)
                    nc.vector.tensor_tensor(xb, xb, ps_w4, ALU.add).then_inc(y_ready, 1)

            def first_windows(layer):
                nc.vector.tensor_copy(win_lo[:, :], chunk_lo[:, :]).then_inc(window_step[layer], 1)
                dve.wait_ge(window_step[layer], 1)
                base_row(layer)

            def edge_sweeps(layer, block_part, parts, last_parts):

                def step(q, i, r, first=False):
                    c = RING * number(i) + r
                    mix(layer, q, i, r)
                    if following(i, r):
                        build_onehot(layer, q, *following(i, r), q * N_CHUNKS + c)
                    if not first:
                        add_window(layer, q, c - 1)

                with dve.Fori(0, n_sweeps) as q:
                    dve.wait_ge(window_ready[layer], q + 1)
                    dve.wait_ge(counted_anew[layer], q + 1)
                    build_onehot(layer, q, 0, 0, q * N_CHUNKS)
                    for s in range(OCTET):
                        step(q, s // RING, s % RING, first=(s == 0))
                    with dve.Fori(1, OCTETS) as p:
                        for s in range(OCTET):
                            step(q, 2 * p + s // RING, s % RING)
                            if s in parts:
                                with dve.If(early > 0):
                                    block_part(s, p - 1)
                    for r in range(RING):
                        step(q, LAST, r)
                        if r in last_parts:
                            with dve.If(early > 0):
                                for s in last_parts[r]:
                                    block_part(s, BLOCKS - LEFT)
                    add_window(layer, q, N_CHUNKS - 1)
                    dve.wait_ge(acc_added[layer], done((q + 1) * N_CHUNKS))
                    nc.vector.tensor_scalar(win_lo[:, :], win_lo[:, :], float(WINDOW), None, ALU.add
                                            ).then_inc(window_step[layer], 1)
                    dve.wait_ge(window_step[layer], q + 2)
                    base_row(layer)
                if layer == 0:
                    dve.wait_ge(window_ready[0], n_sweeps + 1)
                    dve.sem_inc(waited["dve"], 1)
                    first_windows(1)
                with dve.Fori(early * (BLOCKS - 1), BLOCKS) as j:
                    for s in parts:
                        block_part(s, j)

            first_windows(0)
            dve.wait_ge(weights_loaded, 16 * N_WEIGHTS)
            for n in range(PIECES):
                dve.wait_ge(h_ready, act_blocks_done(n))
                if n == PIECES - 1:
                    dve.wait_ge(pool_h_ready, 1)
                    dve.wait_ge(dve_h_ready, 1)
                xv = node_tiles(node_x, n * PIECE_TILES, PIECE_TILES).rearrange("p (j f) -> p j f", f=HID)
                nc.vector.tensor_tensor(xv, xv, b2_s[:, :].unsqueeze(1).broadcast_to([ROWS, PIECE_TILES, HID]),
                                        ALU.add).then_inc(bias_added, 1)
            dve.wait_ge(acc_zeroed, 1)
            dve.wait_ge(zeros_stored, 16)
            dve.wait_ge(bias_added, PIECES)
            edge_sweeps(0, block_part0, (4, 6, 7), {0: (4,), 1: (6, 7)})
            dve.wait_ge(c_ready, done(BLOCKS))
            edge_sweeps(1, block_part1, (4,), {1: (4,)})

        @block.tensor
        def _(pe):
            pe.wait_ge(weights_loaded, 16 * N_WEIGHTS)
            pe.wait_ge(consts_ready, 3)
            pe.wait_ge(ident_ready, 2)
            for layer in range(2):
                pe.sem_inc(summed[layer], RING)
            n_sweeps = sweeps(pe)
            early = steer(pe)

            def turn(q, i, r):
                k, rows = shape_of(i, r)
                g = q * N_CHUNKS + RING * number(i) + r
                pe.wait_ge(turned_copied, done(g))
                pe.wait_ge(onehot_ready[1], g + 1)
                oh = onehot[0:rows, r % 2, 0:k, :].bitcast(BF16)
                for t in range(k):
                    last = nc.tensor.transpose(ps_oht[0:WINDOW, t * rows:(t + 1) * rows],
                                               oh[:, t, 1:2 * WINDOW:2], ident_h[0:rows, 0:rows])
                last.then_inc(turned, 1)

            def products(layer, q, i, r):
                k, rows = shape_of(i, r)
                g = q * N_CHUNKS + RING * number(i) + r
                pe.wait_ge(mixed[layer], done(g))
                if layer == 0:
                    pe.wait_ge(feats_loaded[0][r], 16 * (q * GROUPS + number(i) + 1))
                else:
                    pe.wait_ge(turned_copied, done(g + 1))
                for t in range(k):
                    if layer == 0:
                        last = nc.tensor.matmul(ps_pre[0:rows, t, :], lhs[0:N_RBF, r, t * rows:(t + 1) * rows],
                                                w_rbf_s[:, :], start=True, stop=True)
                    else:
                        last = nc.tensor.matmul(ps_pre[0:rows, t, :], lhs[:, r, t * rows:(t + 1) * rows],
                                                win_b[:, r, :], start=True, stop=True)
                last.then_inc(products_ready[layer], 1)

            def sum_messages(layer, q, i, r):
                k, rows = shape_of(i, r)
                g = q * N_CHUNKS + RING * number(i) + r
                pe.wait_ge(sums_copied[layer], done(g))
                pe.wait_ge(onehot_ready[layer], g + 1)
                if layer:
                    pe.wait_ge(messages_ready, g + 1)
                else:
                    pe.wait_ge(mixed[0], done(g + 1))
                for t in range(k):
                    last = nc.tensor.matmul(ps_sum, gath[0:rows, r, t, :], onehot[0:rows, r % 2, t, :],
                                            start=(t == 0), stop=(t == k - 1))
                if layer == 1:
                    oh = onehot[0:rows, r % 2, 0:k, :].bitcast(BF16)
                    for t in range(k):
                        last = nc.tensor.matmul(ps_deg, ones_h[0:rows, :], oh[:, t, 1:2 * WINDOW:2],
                                                 start=(t == 0), stop=(t == k - 1))
                last.then_inc(summed[layer], 1)

            def project(layer, g):
                pe.wait_ge(sums_copied[layer], done(g + 1))
                pe.wait_ge(acc_added[layer], done(g))
                if layer == 0:
                    nc.tensor.matmul(ps_proj, w1_s[:, :], sums[:, :], start=True, stop=True).then_inc(projected[0], 1)
                    return
                nc.tensor.matmul(ps_proj, m2_s[:, :], sums[:, :], start=True, stop=False)
                nc.tensor.matmul(ps_proj, mb2_s[:, :], deg[:, :], start=False, stop=True).then_inc(projected[1], 1)
                pe.wait_ge(projection_copied, g + 1)
                nc.tensor.matmul(ps_proj2, m3b_s[:, :], sums2[:, :], start=True, stop=True).then_inc(updated, 1)

            def block_product(j, into, weights, finished):
                for t in range(BT):
                    last = nc.tensor.matmul(into[:, t * HID:(t + 1) * HID], u_buf[:, t * ROWS:(t + 1) * ROWS],
                                            weights, start=True, stop=True)
                last.then_inc(finished, 1)

            def turn_h(j):
                pe.wait_ge(x2_ready, done(j + 1))
                pe.wait_ge(h2_ready, j + 1)
                for t in range(BT):
                    last = nc.tensor.transpose(ps_t[:, t * ROWS:(t + 1) * ROWS], h_buf[:, t * HID:(t + 1) * HID],
                                               ident[0:ROWS, 0:ROWS])
                last.then_inc(ht_ready, 1)

            def times_w1(j):
                pe.wait_ge(ht_copied, done(j + 1))
                pe.wait_ge(b_ready, done(j))
                for into, weights, finished in ((ps_a, m1a_s, a_done), (ps_b, m1b_s, b_done)):
                    for t in range(BT):
                        last = nc.tensor.matmul(into[:, t * HID:(t + 1) * HID], ht_buf[:, t * ROWS:(t + 1) * ROWS],
                                                weights[:, :], start=True, stop=True)
                    last.then_inc(finished, 1)

            def times_w3(j):
                pe.wait_ge(c_ready, done(j))
                nc.tensor.matmul(ps_c, m3a_s[:, :], ht_buf, start=True, stop=True).then_inc(c_done, 1)

            def block_part0(s, j):
                if s == 3:
                    pe.wait_ge(u_ready, j + 1)
                    pe.wait_ge(ht_copied, done(j))
                    block_product(j, ps_w2, w2_s[:, :], w2_done)
                if s == 5:
                    turn_h(j)
                if s == 6:
                    times_w1(j)
                if s == 7:
                    times_w3(j)

            def block_part1(s, j):
                if s == 3:
                    pe.wait_ge(v_ready, j + 1)
                    pe.wait_ge(y_ready, done(j))
                    block_product(j, ps_w4, m4_s[:, :], w4_done)

            def edge_sweeps(layer, block_part, parts, last_parts):
                def step(q, i, r, first=False):
                    if not first:
                        project(layer, q * N_CHUNKS + RING * number(i) + r - 1)
                    if layer and following(i, r):
                        turn(q, *following(i, r))
                    sum_messages(layer, q, i, r)
                    if following(i, r):
                        products(layer, q, *following(i, r))

                with pe.Fori(0, n_sweeps) as q:
                    if layer:
                        turn(q, 0, 0)
                    products(layer, q, 0, 0)
                    for s in range(OCTET):
                        step(q, s // RING, s % RING, first=(s == 0))
                    with pe.Fori(1, OCTETS) as p:
                        for s in range(OCTET):
                            step(q, 2 * p + s // RING, s % RING)
                            if s in parts:
                                with pe.If(early > 0):
                                    for part in parts[s]:
                                        block_part(part, p - 1)
                    for r in range(RING):
                        if r in last_parts:
                            with pe.If(early > 0):
                                for s in last_parts[r]:
                                    block_part(s, BLOCKS - LEFT)
                        step(q, LAST, r)
                    project(layer, (q + 1) * N_CHUNKS - 1)
                with pe.Fori(early * (BLOCKS - 1), BLOCKS) as j:
                    for s in parts:
                        for part in parts[s]:
                            block_part(part, j)

            edge_sweeps(0, block_part0, {3: (3,), 5: (5,), 6: (6, 7)}, {0: (3,), 1: (5, 6), 3: (7,)})
            edge_sweeps(1, block_part1, {3: (3,)}, {0: (3,)})


def kernel(**inputs):
    import concourse.bacc as _bacc
    from concourse.bass_utils import run_bass_kernel_spmd as _run

    a = {k: np.asarray(v) for k, v in inputs.items()}
    full = FULL * CHUNK

    def by_chunk(v):
        return v[:full].reshape(FULL * P, K), v[full:].reshape(TAIL_ROWS, TAIL_K)

    def features(v):
        n = v.shape[1]
        body = v[:full].reshape(FULL, P, K, n).transpose(0, 3, 2, 1).reshape(FULL * n, CHUNK)
        tail = v[full:].reshape(TAIL_ROWS, TAIL_K, n).transpose(2, 1, 0).reshape(n, TAIL)
        return body, tail

    (src, src_tail), (dst, dst_tail) = by_chunk(a["src"]), by_chunk(a["dst"])
    rbf, rbf_tail = features(a["edge_attr_6"])
    ef, ef_tail = features(a["edge_attr_16"])
    laid = {
        "x": a["x"], "dst": a["dst"],
        "ids": np.concatenate([src, dst], axis=1), "ids_tail": np.concatenate([src_tail, dst_tail], axis=1),
        "rbf": rbf, "rbf_tail": rbf_tail, "ef": ef, "ef_tail": ef_tail,
        "w_rbf_t": a["L0_gnn_W_rbf"].T, "w1_t": a["L0_gnn_W1"].T, "b1": a["L0_gnn_b1"][:, None],
        "w2_t": a["L0_gnn_W2"].T, "b2": a["L0_gnn_b2"][None, :],
        "m1": a["L1_gnn_W1"], "mb1": a["L1_gnn_b1"][None, :], "m2": a["L1_gnn_W2"], "mb2": a["L1_gnn_b2"][None, :],
        "m3": a["L1_gnn_W3"], "mb3": a["L1_gnn_b3"][:, None], "m4": a["L1_gnn_W4"], "mb4": a["L1_gnn_b4"][None, :],
    }
    nc = _bacc.Bacc("TRN2", target_bir_lowering=False, num_devices=1)
    arrays, args = {}, []
    for name, v in laid.items():
        v = np.ascontiguousarray(v)
        arrays[f"in_{name}"] = v
        args.append(nc.dram_tensor(f"in_{name}", v.shape, mybir.dt.from_np(v.dtype), kind="ExternalInput").ap())
    out = nc.dram_tensor("out_0", (N_NODES, HID), F32, kind="ExternalOutput").ap()
    gnn_kernel(nc, *args, out)
    r = _run(nc, [arrays], core_ids=[0])
    return r.results[0]["out_0"]
```
